# Optimizing a Trainium2 kernel written in Bass

```python
import numpy as np
import jax
import jax.numpy as jnp

def _softmax(x, axis=-1):
    return jax.nn.softmax(x, axis=axis)

def _gelu(x):
    return jax.nn.gelu(x, approximate=True)

def _silu(x):
    return jax.nn.silu(x)

def _sigmoid(x):
    return jax.nn.sigmoid(x)

def _layernorm(x, axis=-1, eps=1e-05):
    m = jnp.mean(x, axis=axis, keepdims=True)
    v = jnp.var(x, axis=axis, keepdims=True)
    return (x - m) / jnp.sqrt(v + eps)

def _scatter_add(tgt, idx, src, axis=0):
    return tgt.at[idx].add(src)

def _segment_sum(src, seg, n):
    return jax.ops.segment_sum(src, seg, n)
kernel_name = 'mk_gnn_preln_d4_gnn_r64_d40c9b'

def setup_inputs(seed: int=0):
    np.random.seed(seed)
    _w = jnp.asarray

    def _rec_inputs():
        import jax
        import jax.numpy as jnp
        _gk = jax.random.key(seed)
        x = -0.000202 + 1 * jax.random.normal(jax.random.fold_in(_gk, 1), (100000, 64), jnp.float32)
        src = jax.random.randint(jax.random.fold_in(_gk, 2), (50000,), 0, 100000, jnp.int32)
        dst = jax.random.randint(jax.random.fold_in(_gk, 3), (50000,), 0, 100000, jnp.int32)
        _o = jnp.argsort(dst, stable=True)
        src = src[_o]
        dst = dst[_o]
        edge_attr_16 = 0.000254156 + 0.999948 * jax.random.normal(jax.random.fold_in(_gk, 12), (50000, 16), jnp.float32)
        edge_attr_18 = 0.000175535 + 1.00015 * jax.random.normal(jax.random.fold_in(_gk, 13), (50000, 18), jnp.float32)
        edge_type_3 = jax.random.randint(jax.random.fold_in(_gk, 15), (50000,), 0, 3, jnp.int32)
        edge_weight = jax.random.uniform(jax.random.fold_in(_gk, 16), (50000,), jnp.float32, 0.0, 1)
        return (x, src, dst, edge_attr_16, edge_attr_18, edge_type_3, edge_weight)
    x, src, dst, edge_attr_16, edge_attr_18, edge_type_3, edge_weight = _rec_inputs()

    def _L0_gnn_setup():
        import jax, jax.numpy as jnp
        import numpy as np
        N_NODES = 100000
        NEG_SLOPE = 0.2
        EPS = 1e-16
        key = jax.random.key(seed)
        k1, k2, k3, k4 = jax.random.split(key, 4)
        in_dim, out_dim, n_edges = (64, 64, 25000)
        x = jax.random.normal(k1, (N_NODES, in_dim), dtype=jnp.float32)
        edge_index = jax.random.randint(k2, (2, n_edges), 0, N_NODES, dtype=jnp.int64)
        W = jax.random.normal(k3, (in_dim, out_dim), dtype=jnp.float32) / np.sqrt(in_dim)
        ka, kb = jax.random.split(k4)
        att_src = jax.random.normal(ka, (out_dim,), dtype=jnp.float32) / np.sqrt(out_dim)
        att_dst = jax.random.normal(kb, (out_dim,), dtype=jnp.float32) / np.sqrt(out_dim)
        bias = jnp.zeros((out_dim,), dtype=jnp.float32)
        return {'x': x, 'edge_index': edge_index, 'W': W, 'att_src': att_src, 'att_dst': att_dst, 'bias': bias}
    _L0_gnn_all = _L0_gnn_setup()
    _L0_gnn_in = {k: v for k, v in _L0_gnn_all.items() if k in ('W', 'att_src', 'att_dst', 'bias')}
    del _L0_gnn_all

    def _L1_gnn_setup():
        import jax, jax.numpy as jnp
        import numpy as np
        N, E = (50000, 12500)
        NODE_DIM, EDGE_DIM, HEADS = (64, 16, 4)
        C = NODE_DIM // HEADS
        NEG_SLOPE = 0.2
        BN_EPS = 1e-05
        key = jax.random.key(seed)
        ks = jax.random.split(key, 12)
        glorot = lambda k, shape: jax.random.normal(k, shape, jnp.float32) * np.sqrt(2.0 / (shape[0] + shape[-1]))
        return {'x': jax.random.normal(ks[0], (N, NODE_DIM), jnp.float32), 'edge_index': jax.random.randint(ks[1], (2, E), 0, N, jnp.int32), 'edge_attr': jax.random.normal(ks[2], (E, EDGE_DIM), jnp.float32), 'W_l': glorot(ks[3], (NODE_DIM, HEADS * C)), 'b_l': jnp.zeros((HEADS * C,), jnp.float32), 'W_r': glorot(ks[4], (NODE_DIM, HEADS * C)), 'b_r': jnp.zeros((HEADS * C,), jnp.float32), 'W_e': glorot(ks[5], (EDGE_DIM, HEADS * C)), 'att': glorot(ks[6], (HEADS, C)), 'bias': jnp.zeros((HEADS * C,), jnp.float32), 'gamma': jnp.ones((NODE_DIM,), jnp.float32), 'beta': jnp.zeros((NODE_DIM,), jnp.float32)}
    _L1_gnn_all = _L1_gnn_setup()
    _L1_gnn_in = {k: v for k, v in _L1_gnn_all.items() if k in ('W_l', 'b_l', 'W_r', 'b_r', 'W_e', 'att', 'bias', 'gamma', 'beta')}
    del _L1_gnn_all

    def _L2_gnn_setup():
        import jax, jax.numpy as jnp
        import numpy as np
        N = 100000
        E = 25000
        DIM = 64
        H = 4
        D = 8
        DH = D * H
        VD = DIM // H
        RPE_IN = 18
        key = jax.random.key(seed)
        ks = jax.random.split(key, 12)
        x = jax.random.normal(ks[0], (N, DIM), dtype=jnp.float32)
        edge_index = jax.random.randint(ks[1], (2, E), 0, N, dtype=jnp.int64)
        edge_attr = jax.random.normal(ks[2], (E, RPE_IN), dtype=jnp.float32)
        sc = lambda fan_in: 1.0 / np.sqrt(fan_in)
        qkv_w = jax.random.uniform(ks[3], (DIM, 2 * DH + DIM), jnp.float32, -sc(DIM), sc(DIM))
        qkv_b = jax.random.uniform(ks[4], (2 * DH + DIM,), jnp.float32, -sc(DIM), sc(DIM))
        k_rpe_w = jax.random.uniform(ks[5], (RPE_IN, DH), jnp.float32, -sc(RPE_IN), sc(RPE_IN))
        k_rpe_b = jax.random.uniform(ks[6], (DH,), jnp.float32, -sc(RPE_IN), sc(RPE_IN))
        q_rpe_w = jax.random.uniform(ks[7], (RPE_IN, DH), jnp.float32, -sc(RPE_IN), sc(RPE_IN))
        q_rpe_b = jax.random.uniform(ks[8], (DH,), jnp.float32, -sc(RPE_IN), sc(RPE_IN))
        v_rpe_w = jax.random.uniform(ks[9], (RPE_IN, DIM), jnp.float32, -sc(RPE_IN), sc(RPE_IN))
        v_rpe_b = jax.random.uniform(ks[10], (DIM,), jnp.float32, -sc(RPE_IN), sc(RPE_IN))
        return {'x': x, 'edge_index': edge_index, 'edge_attr': edge_attr, 'qkv_w': qkv_w, 'qkv_b': qkv_b, 'k_rpe_w': k_rpe_w, 'k_rpe_b': k_rpe_b, 'q_rpe_w': q_rpe_w, 'q_rpe_b': q_rpe_b, 'v_rpe_w': v_rpe_w, 'v_rpe_b': v_rpe_b}
    _L2_gnn_all = _L2_gnn_setup()
    _L2_gnn_in = {k: v for k, v in _L2_gnn_all.items() if k in ('qkv_w', 'qkv_b', 'k_rpe_w', 'k_rpe_b', 'q_rpe_w', 'q_rpe_b', 'v_rpe_w', 'v_rpe_b')}
    del _L2_gnn_all

    def _L3_gnn_setup():
        import jax, jax.numpy as jnp
        import numpy as np
        N_NODES = 100000
        N_EDGES = 15625
        D = 64
        NUM_LAYERS = 2
        NUM_REL = 3
        BN_EPS = 1e-05

        def _gru_cell(x, h, w_ih, w_hh, b_ih, b_hh):
            gi = x @ w_ih.T + b_ih
            gh = h @ w_hh.T + b_hh
            i_r, i_z, i_n = jnp.split(gi, 3, axis=-1)
            h_r, h_z, h_n = jnp.split(gh, 3, axis=-1)
            r = jax.nn.sigmoid(i_r + h_r)
            z = jax.nn.sigmoid(i_z + h_z)
            n = jnp.tanh(i_n + r * h_n)
            return (1.0 - z) * n + z * h
        key = jax.random.key(seed)
        ks = jax.random.split(key, 10)
        h = jax.random.normal(ks[0], (N_NODES, D), dtype=jnp.float32)
        norm = jax.random.uniform(ks[1], (N_EDGES,), dtype=jnp.float32)
        src = jax.random.randint(ks[2], (N_EDGES,), 0, N_NODES, dtype=jnp.int32)
        dst = jax.random.randint(ks[3], (N_EDGES,), 0, N_NODES, dtype=jnp.int32)
        rel_type = jax.random.randint(ks[4], (N_EDGES,), 0, NUM_REL, dtype=jnp.int32)
        bound = np.sqrt(6.0 / D)
        weight = jax.random.uniform(ks[5], (NUM_REL, D, D), minval=-bound, maxval=bound, dtype=jnp.float32)
        s = 1.0 / np.sqrt(D)
        w_ih = jax.random.uniform(ks[6], (3 * D, D), minval=-s, maxval=s, dtype=jnp.float32)
        w_hh = jax.random.uniform(ks[7], (3 * D, D), minval=-s, maxval=s, dtype=jnp.float32)
        b_ih = jax.random.uniform(ks[8], (3 * D,), minval=-s, maxval=s, dtype=jnp.float32)
        b_hh = jax.random.uniform(ks[9], (3 * D,), minval=-s, maxval=s, dtype=jnp.float32)
        gamma = jnp.ones((D,), dtype=jnp.float32)
        beta = jnp.zeros((D,), dtype=jnp.float32)
        return {'h': h, 'norm': norm, 'weight': weight, 'w_ih': w_ih, 'w_hh': w_hh, 'b_ih': b_ih, 'b_hh': b_hh, 'gamma': gamma, 'beta': beta, 'src': src, 'dst': dst, 'rel_type': rel_type}
    _L3_gnn_all = _L3_gnn_setup()
    _L3_gnn_in = {k: v for k, v in _L3_gnn_all.items() if k in ('weight', 'w_ih', 'w_hh', 'b_ih', 'b_hh', 'gamma', 'beta')}
    del _L3_gnn_all
    return {'x': x, 'src': src, 'dst': dst, 'edge_attr_16': edge_attr_16, 'edge_attr_18': edge_attr_18, 'edge_type_3': edge_type_3, 'edge_weight': edge_weight, 'L0_gnn_W': _L0_gnn_in['W'], 'L0_gnn_att_src': _L0_gnn_in['att_src'], 'L0_gnn_att_dst': _L0_gnn_in['att_dst'], 'L0_gnn_bias': _L0_gnn_in['bias'], 'L1_gnn_W_l': _L1_gnn_in['W_l'], 'L1_gnn_b_l': _L1_gnn_in['b_l'], 'L1_gnn_W_r': _L1_gnn_in['W_r'], 'L1_gnn_b_r': _L1_gnn_in['b_r'], 'L1_gnn_W_e': _L1_gnn_in['W_e'], 'L1_gnn_att': _L1_gnn_in['att'], 'L1_gnn_bias': _L1_gnn_in['bias'], 'L1_gnn_gamma': _L1_gnn_in['gamma'], 'L1_gnn_beta': _L1_gnn_in['beta'], 'L2_gnn_qkv_w': _L2_gnn_in['qkv_w'], 'L2_gnn_qkv_b': _L2_gnn_in['qkv_b'], 'L2_gnn_k_rpe_w': _L2_gnn_in['k_rpe_w'], 'L2_gnn_k_rpe_b': _L2_gnn_in['k_rpe_b'], 'L2_gnn_q_rpe_w': _L2_gnn_in['q_rpe_w'], 'L2_gnn_q_rpe_b': _L2_gnn_in['q_rpe_b'], 'L2_gnn_v_rpe_w': _L2_gnn_in['v_rpe_w'], 'L2_gnn_v_rpe_b': _L2_gnn_in['v_rpe_b'], 'L3_gnn_weight': _L3_gnn_in['weight'], 'L3_gnn_w_ih': _L3_gnn_in['w_ih'], 'L3_gnn_w_hh': _L3_gnn_in['w_hh'], 'L3_gnn_b_ih': _L3_gnn_in['b_ih'], 'L3_gnn_b_hh': _L3_gnn_in['b_hh'], 'L3_gnn_gamma': _L3_gnn_in['gamma'], 'L3_gnn_beta': _L3_gnn_in['beta']}

def reference(x, src, dst, edge_attr_16, edge_attr_18, edge_type_3, edge_weight, L0_gnn_W, L0_gnn_att_src, L0_gnn_att_dst, L0_gnn_bias, L1_gnn_W_l, L1_gnn_b_l, L1_gnn_W_r, L1_gnn_b_r, L1_gnn_W_e, L1_gnn_att, L1_gnn_bias, L1_gnn_gamma, L1_gnn_beta, L2_gnn_qkv_w, L2_gnn_qkv_b, L2_gnn_k_rpe_w, L2_gnn_k_rpe_b, L2_gnn_q_rpe_w, L2_gnn_q_rpe_b, L2_gnn_v_rpe_w, L2_gnn_v_rpe_b, L3_gnn_weight, L3_gnn_w_ih, L3_gnn_w_hh, L3_gnn_b_ih, L3_gnn_b_hh, L3_gnn_gamma, L3_gnn_beta):
    import jax
    import jax.numpy as jnp

    def _L0_gnn_ref(x, edge_index, W, att_src, att_dst, bias):
        import jax, jax.numpy as jnp
        import numpy as np
        N_NODES = 100000
        NEG_SLOPE = 0.2
        EPS = 1e-16
        src, dst = (edge_index[0], edge_index[1])
        h = x @ W
        a_src = h @ att_src
        a_dst = h @ att_dst
        e = jax.nn.leaky_relu(a_src[src] + a_dst[dst], NEG_SLOPE)
        m = jax.ops.segment_max(e, dst, num_segments=N_NODES)
        e = jnp.exp(e - m[dst])
        denom = jax.ops.segment_sum(e, dst, num_segments=N_NODES)
        alpha = e / (denom[dst] + EPS)
        out = jax.ops.segment_sum(alpha[:, None] * h[src], dst, num_segments=N_NODES)
        return jnp.tanh(out + bias)

    def _L1_gnn_ref(x, edge_index, edge_attr, W_l, b_l, W_r, b_r, W_e, att, bias, gamma, beta):
        import jax, jax.numpy as jnp
        import numpy as np
        N, E = (50000, 12500)
        NODE_DIM, EDGE_DIM, HEADS = (64, 16, 4)
        C = NODE_DIM // HEADS
        NEG_SLOPE = 0.2
        BN_EPS = 1e-05
        src, dst = (edge_index[0], edge_index[1])
        n = x.shape[0]
        xl = (x @ W_l + b_l).reshape(n, HEADS, C)
        xr = (x @ W_r + b_r).reshape(n, HEADS, C)
        e = (edge_attr @ W_e).reshape(-1, HEADS, C)
        g = jax.nn.leaky_relu(xl[src] + xr[dst] + e, NEG_SLOPE)
        logits = jnp.einsum('ehc,hc->eh', g, att)
        amax = jax.ops.segment_max(logits, dst, num_segments=n)
        ex = jnp.exp(logits - amax[dst])
        denom = jax.ops.segment_sum(ex, dst, num_segments=n)
        alpha = ex / (denom[dst] + 1e-16)
        msg = xl[src] * alpha[..., None]
        out = jax.ops.segment_sum(msg, dst, num_segments=n).reshape(n, HEADS * C) + bias
        mean = out.mean(axis=0)
        var = out.var(axis=0)
        out = (out - mean) * jax.lax.rsqrt(var + BN_EPS) * gamma + beta
        return jax.nn.gelu(out + x, approximate=False)

    def _L2_gnn_ref(x, edge_index, edge_attr, qkv_w, qkv_b, k_rpe_w, k_rpe_b, q_rpe_w, q_rpe_b, v_rpe_w, v_rpe_b):
        import jax, jax.numpy as jnp
        import numpy as np
        N = 100000
        E = 25000
        DIM = 64
        H = 4
        D = 8
        DH = D * H
        VD = DIM // H
        RPE_IN = 18
        n = x.shape[0]
        e = edge_index.shape[1]
        qkv = x @ qkv_w + qkv_b
        q = qkv[:, :DH].reshape(n, H, D)
        k = qkv[:, DH:2 * DH].reshape(n, H, D)
        v = qkv[:, 2 * DH:].reshape(n, H, VD)
        s = edge_index[0]
        t = edge_index[1]
        scale = jnp.float32(D) ** (-0.5)
        qe = q[s] * scale
        qe = qe + (edge_attr @ q_rpe_w + q_rpe_b).reshape(e, H, D)
        ke = k[t] + (edge_attr @ k_rpe_w + k_rpe_b).reshape(e, H, D)
        ve = v[t] + (edge_attr @ v_rpe_w + v_rpe_b).reshape(e, H, VD)
        compat = jnp.einsum('ehd,ehd->eh', qe, ke)
        m = jax.ops.segment_max(compat, s, num_segments=n)
        ex = jnp.exp(compat - m[s])
        den = jax.ops.segment_sum(ex, s, num_segments=n)
        attn = ex / (den[s] + 1e-16)
        msg = (ve * attn[..., None]).reshape(e, DIM)
        out = jax.ops.segment_sum(msg, s, num_segments=n)
        return out

    def _L3_gnn_ref(h, norm, weight, w_ih, w_hh, b_ih, b_hh, gamma, beta, src, dst, rel_type):
        import jax, jax.numpy as jnp
        import numpy as np
        N_NODES = 100000
        N_EDGES = 15625
        D = 64
        NUM_LAYERS = 2
        NUM_REL = 3
        BN_EPS = 1e-05

        def _gru_cell(x, h, w_ih, w_hh, b_ih, b_hh):
            gi = x @ w_ih.T + b_ih
            gh = h @ w_hh.T + b_hh
            i_r, i_z, i_n = jnp.split(gi, 3, axis=-1)
            h_r, h_z, h_n = jnp.split(gh, 3, axis=-1)
            r = jax.nn.sigmoid(i_r + h_r)
            z = jax.nn.sigmoid(i_z + h_z)
            n = jnp.tanh(i_n + r * h_n)
            return (1.0 - z) * n + z * h
        output = h
        hstate = jnp.zeros_like(h)
        for _ in range(NUM_LAYERS):
            t = jnp.einsum('nd,rde->rne', output, weight)
            msg = t[rel_type, src] * norm[:, None]
            swh = jax.ops.segment_sum(msg, dst, num_segments=N_NODES)
            hstate = _gru_cell(swh, hstate, w_ih, w_hh, b_ih, b_hh)
            output = hstate
        mean = jnp.mean(output, axis=0)
        var = jnp.mean(jnp.square(output - mean), axis=0)
        return (output - mean) / jnp.sqrt(var + BN_EPS) * gamma + beta
    edge_index = jnp.stack([src, dst])
    h = jnp.maximum(_layernorm(x, axis=-1), 0.0)
    x = x + _L0_gnn_ref(h, edge_index, L0_gnn_W, L0_gnn_att_src, L0_gnn_att_dst, L0_gnn_bias)
    h = jnp.maximum(_layernorm(x, axis=-1), 0.0)
    x = x + _L1_gnn_ref(h, edge_index, edge_attr_16, L1_gnn_W_l, L1_gnn_b_l, L1_gnn_W_r, L1_gnn_b_r, L1_gnn_W_e, L1_gnn_att, L1_gnn_bias, L1_gnn_gamma, L1_gnn_beta)
    h = jnp.maximum(_layernorm(x, axis=-1), 0.0)
    x = x + _L2_gnn_ref(h, edge_index, edge_attr_18, L2_gnn_qkv_w, L2_gnn_qkv_b, L2_gnn_k_rpe_w, L2_gnn_k_rpe_b, L2_gnn_q_rpe_w, L2_gnn_q_rpe_b, L2_gnn_v_rpe_w, L2_gnn_v_rpe_b)
    h = jnp.maximum(_layernorm(x, axis=-1), 0.0)
    x = x + _L3_gnn_ref(h, edge_weight, L3_gnn_weight, L3_gnn_w_ih, L3_gnn_w_hh, L3_gnn_b_ih, L3_gnn_b_hh, L3_gnn_gamma, L3_gnn_beta, src, dst, edge_type_3)
    return x

_drawn_inputs = setup_inputs


def setup_inputs(seed=0):
    import zlib

    import numpy as np

    out = dict(_drawn_inputs(seed))
    spreads = {'L0_gnn_bias': (0.0, 0.1),
     'L1_gnn_b_l': (0.0, 0.1),
     'L1_gnn_b_r': (0.0, 2.0),
     'L1_gnn_bias': (0.0, 2.0),
     'L1_gnn_gamma': (1.0, 0.2),
     'L1_gnn_beta': (0.0, 0.1),
     'L3_gnn_gamma': (1.0, 0.2),
     'L3_gnn_beta': (0.0, 0.1)}
    factors = {'L0_gnn_att_src': 3.098,
     'L0_gnn_att_dst': 21.517,
     'L2_gnn_k_rpe_b': 3.805,
     'L2_gnn_q_rpe_b': 4.132,
     'L1_gnn_W_r': 2.988}
    for name, (base, spread) in spreads.items():
        noise = np.random.default_rng([zlib.crc32(name.encode()), seed]).standard_normal(out[name].shape)
        drawn = base * np.exp(spread * noise) if base else spread * noise
        out[name] = jnp.asarray(drawn.astype(out[name].dtype))
    for name, factor in factors.items():
        out[name] = (out[name] * factor).astype(out[name].dtype)
    return out
```

```python
from contextlib import ExitStack

import concourse.bass as bass
from concourse import mybir

F32 = mybir.dt.float32
I32 = mybir.dt.int32
ALU = mybir.AluOpType
ACT = mybir.ActivationFunctionType
AX = mybir.AxisListType.X

P = 128
D = 64
TPC = 4
CE = TPC * P
NBLK = 4
LIST = NBLK * P * P
PAD_NODE = 131071
SKIP = 1 << 20
FAR = -1.0e30
LN_EPS = 1e-5
NR = 8


class Scope:

    def __init__(self, nc, name):
        self.nc, self.name, self.stack, self.used = nc, name, ExitStack(), []

    whole = None

    def __enter__(self):
        self.stack.__enter__()
        return self

    def __exit__(self, *a):
        if self.used and a[0] is None:
            with self.nc.Block() as block:
                @block.gpsimd
                def _(pool):
                    for s in self.used:
                        pool.sem_clear(s)
        return self.stack.__exit__(*a)

    def sb(self, name, shape, dt=F32):
        return self.stack.enter_context(self.nc.sbuf_tensor(f"{self.name}_{name}", shape, dt))

    def ps(self, name, shape=(P, CE)):
        return self.stack.enter_context(self.nc.psum_tensor(f"{self.name}_{name}", list(shape), F32))

    def sem(self, name):
        s = self.stack.enter_context(self.nc.semaphore(f"{self.name}_{name}"))
        self.used.append(s)
        return s

    def swdge_sem(self, name):
        return Scope.whole.stack.enter_context(self.nc.semaphore(f"{self.name}_{name}"))

    def sems(self, names):
        return {n: self.sem(n) for n in names.split()}


class Chain:

    def __init__(self, eng, sem):
        self.eng, self.sem, self.n = eng, sem, 0

    def restart(self, first):
        if self.n or not first:
            self.eng.sem_clear(self.sem)
        self.n = 0

    def __call__(self, ins):
        self.n += 1
        ins.then_inc(self.sem, 1)
        self.eng.wait_ge(self.sem, self.n)
        return ins



def turns(eng, n, body):
    body(0, True, False)
    with eng.Fori(1, n - 1) as t:
        body(t, False, False)
    body(n - 1, False, True)


def bc(ap, shape):
    return ap.to_broadcast(shape)


def hold(eng, sem, n):
    eng.wait_ge(sem, n)
    eng.nop(nofuse=True)


def prep_lists(nc, c, src, dst, weight, etype, dram):
    E = src.shape[0]
    N = c.N
    full, rest = E // P, E % P
    blocks = [min(P, full - b * P) for b in range(NBLK)]
    with Scope(nc, "prep") as s:
        ident = c.ident
        key = [s.sb(f"key{i}", [P, NBLK * P]) for i in range(2)]
        pay = [s.sb(f"pay{i}", [P, NBLK * P]) for i in range(2)]
        swap = s.sb("swap", [P, NBLK * P // 2], I32)
        icur = s.sb("icur", [P, NBLK, P], I32)
        iprev = s.sb("iprev", [P, NBLK, P], I32)
        inext = s.sb("inext", [P, NBLK, P], I32)
        isrc = s.sb("isrc", [P, NBLK, P], I32)
        ityp = s.sb("ityp", [P, NBLK, P], I32)
        nrm = s.sb("nrm", [P, NBLK, P])
        idx_i = s.sb("idx_i", [P, NBLK * P], I32)
        cur = s.sb("cur", [P, NBLK, P])
        oth = s.sb("oth", [P, NBLK, P])
        start = s.sb("start", [P, NBLK, P])
        flag = s.sb("flag", [P, NBLK, P])
        sgn = s.sb("sgn", [P, 1])
        sgn_i = s.sb("sgn_i", [P, 1], I32)
        ptk, ptp = s.ps("ptk"), s.ps("ptp")
        filled, loaded, keys_ready, pay_copied = (s.sem(n) for n in ("filled", "loaded", "keys_ready", "pay_copied"))
        dve_step, turned, stored, last_pay, to_store = (s.sem(n) for n in ("dve_step", "turned", "stored", "last_pay", "to_store"))
        keys_stored, keys_back, pool_step = s.sem("keys_stored"), s.sem("keys_back"), s.sem("pool_step")

        levels = [(k, j) for k in range(1, 17) for j in range(k - 1, -1, -1)]
        n_stage = len(levels)
        with nc.Block() as block:

            @block.gpsimd
            def _(pool):
                pool.memset(icur[:], PAD_NODE).then_inc(filled, 1)
                pool.memset(iprev[:], PAD_NODE).then_inc(filled, 1)
                pool.memset(inext[:], PAD_NODE).then_inc(filled, 1)
                pool.memset(isrc[:], PAD_NODE).then_inc(filled, 1)
                pool.memset(ityp[:], 0).then_inc(filled, 1)
                pool.memset(nrm[:], 0.0).then_inc(filled, 1)
                pool.iota(idx_i[:].rearrange("p (b f) -> p b f", b=NBLK), pattern=[[P * P, NBLK], [1, P]],
                          base=0, channel_multiplier=P).then_inc(filled, 1)
                pool.iota(sgn_i[:], pattern=[[0, 1]], base=0, channel_multiplier=1).then_inc(filled, 1)
                pool.wait_ge(filled, 8)
                pool.memset(iprev[0:1, 0, 0:1], -1).then_inc(filled, 1)

            loads = []

            @block.sync
            def _(sp):
                sp.wait_ge(filled, 9)
                n = 0
                for tile_, vec in ((isrc, src), (icur, dst), (ityp, etype), (nrm, weight)):
                    for b, rows in enumerate(blocks):
                        sp.dma_start(tile_[0:rows, b, :], vec[b * P * P:b * P * P + rows * P].rearrange("(r f) -> r f", f=P)).then_inc(loaded, 16)
                        n += 1
                    sp.dma_start(tile_[blocks[-1]:blocks[-1] + 1, NBLK - 1, 0:rest], vec[full * P:E].rearrange("(r f) -> r f", r=1)).then_inc(loaded, 16)
                    n += 1
                for b, rows in enumerate(blocks):
                    sp.dma_start(inext[0:rows, b, :], dst[b * P * P + 1:b * P * P + rows * P + 1].rearrange("(r f) -> r f", f=P)).then_inc(loaded, 16)
                    lo = 1 if b == 0 else 0
                    sp.dma_start(iprev[lo:rows, b, :], dst[(b * P + lo) * P - 1:(b * P + rows) * P - 1].rearrange("(r f) -> r f", f=P)).then_inc(loaded, 16)
                    n += 2
                sp.dma_start(iprev[0:1, 0, 1:P], dst[0:P - 1].rearrange("(r f) -> r f", r=1)).then_inc(loaded, 16)
                sp.dma_start(inext[blocks[-1]:blocks[-1] + 1, NBLK - 1, 0:rest - 1], dst[full * P + 1:E].rearrange("(r f) -> r f", r=1)).then_inc(loaded, 16)
                sp.dma_start(iprev[blocks[-1]:blocks[-1] + 1, NBLK - 1, 0:rest], dst[full * P - 1:E - 1].rearrange("(r f) -> r f", r=1)).then_inc(loaded, 16)
                loads.append(n + 3)
                sp.wait_ge(to_store, 1)
                sp.dma_start(dram["far_d"].rearrange("(b p f) -> p b f", p=P, f=P), start[:]).then_inc(stored, 16)
                sp.dma_start(dram["keep_d"].rearrange("(b p f) -> p b f", p=P, f=P), flag[:]).then_inc(stored, 16)
                sp.wait_ge(to_store, 2)
                sp.dma_start(dram["keys"][1:LIST + 1].rearrange("(b p f) -> p b f", p=P, f=P), cur[:]).then_inc(keys_stored, 16)
                sp.dma_start(dram["keys"][0:1].rearrange("(r f) -> r f", r=1), c.minus1[0:1, 0:1]).then_inc(keys_stored, 16)
                sp.dma_start(dram["keys"][LIST + 1:LIST + 2].rearrange("(r f) -> r f", r=1), c.minus1[0:1, 0:1]).then_inc(keys_stored, 16)
                sp.wait_ge(keys_stored, 48)
                sp.dma_start(oth[:], dram["keys"][0:LIST].rearrange("(b p f) -> p b f", p=P, f=P)).then_inc(keys_back, 16)
                sp.dma_start(nrm[:], dram["keys"][2:LIST + 2].rearrange("(b p f) -> p b f", p=P, f=P)).then_inc(keys_back, 16)
                sp.wait_ge(to_store, 3)
                sp.dma_start(dram["far_s"].rearrange("(b p f) -> p b f", p=P, f=P), start[:]).then_inc(stored, 16)
                sp.wait_ge(stored, 48)

            @block.scalar
            def _(act):
                for n in range(n_stage):
                    act.wait_ge(keys_ready, n + 1)
                    act.activation(pay[(n + 1) % 2][:], pay[n % 2][:], ACT.Copy).then_inc(pay_copied, 1)

            @block.vector
            def _(dve):
                step = Chain(dve, dve_step)
                flips = [0]

                def turned_rows(view_in, out):
                    flips[0] += 1
                    dve.wait_ge(turned, flips[0])
                    step(dve.tensor_copy(out, ptk[:]))

                dve.wait_ge(loaded, 16 * loads[0])
                dve.wait_ge(filled, 9)
                flat = lambda a: a[:].rearrange("p b f -> p (b f)")
                step(dve.tensor_copy(flat(cur), flat(icur)))
                step(dve.tensor_copy(flat(oth), flat(iprev)))
                step(dve.tensor_tensor(flat(start), flat(cur), flat(oth), ALU.not_equal))
                step(dve.tensor_scalar(flat(flag), flat(start), -1.0, 1.0, ALU.mult, ALU.add))
                step(dve.tensor_scalar(flat(start), flat(start), FAR, None, ALU.mult))
                dve.sem_inc(to_store, 1)
                step(dve.tensor_copy(flat(oth), flat(inext)))
                step(dve.tensor_tensor(key[1][:], flat(cur), flat(oth), ALU.not_equal))

                def to_columns(rows, out):
                    flips[0] += 1
                    step(dve.tensor_copy(pay[1][:], rows))
                    dve.sem_inc(last_pay, 1)
                    dve.wait_ge(turned, flips[0])
                    step(dve.tensor_copy(out, ptk[:, 0:c.NT] if out.shape[-1] == c.NT else ptk[:]))

                to_columns(key[1][:], c.last_d[:])
                step(dve.tensor_scalar(key[0][:], key[1][:], -float(SKIP), float(SKIP), ALU.mult, ALU.add))
                step(dve.tensor_tensor(key[0][:], key[0][:], flat(cur), ALU.add))
                to_columns(key[0][:], c.scat_d[:])
                for lst, out in ((icur, c.idx_dst), (isrc, c.idx_src)):
                    step(dve.tensor_copy(key[0][:], flat(lst)))
                    step(dve.tensor_scalar(key[1][:], key[0][:], float(N) - 0.5, None, ALU.is_lt))
                    step(dve.tensor_tensor(key[0][:], key[0][:], key[1][:], ALU.mult))
                    to_columns(key[0][:], out[:])
                for r in range(c.NREL):
                    step(dve.tensor_copy(key[0][:], flat(ityp)))
                    step(dve.tensor_scalar(key[0][:], key[0][:], float(r), None, ALU.is_equal))
                    step(dve.tensor_tensor(key[0][:], key[0][:], flat(nrm), ALU.mult))
                    to_columns(key[0][:], c.wrel[:, :, r])

                step(dve.tensor_copy(key[0][:], flat(isrc)))
                step(dve.tensor_copy(pay[0][:], idx_i[:]))
                step(dve.tensor_scalar(sgn_i[:], sgn_i[:], 1, None, ALU.bitwise_and))
                step(dve.tensor_scalar(sgn[:], sgn_i[:], -2.0, 1.0, ALU.mult, ALU.add))

                def descending(k, at, layout):
                    if k == 16:
                        return
                    if k == 7:
                        step(dve.tensor_scalar(at[:], at[:], sgn[:, 0:1], None, ALU.mult))
                        return
                    d = 1 << (k if layout == "T" else k - 7)
                    v = at[:].rearrange("p (n two d) -> p n two d", two=2, d=d)[:, :, 1, :]
                    step(dve.tensor_scalar(v, v, -1.0, None, ALU.mult))

                layout = "T"
                for n, (k, j) in enumerate(levels):
                    kin, kout, pin, pout = key[n % 2], key[(n + 1) % 2], pay[n % 2], pay[(n + 1) % 2]
                    need = "T" if j < 7 else "A"
                    if need != layout:
                        dve.sem_inc(last_pay, 1)
                        flips[0] += 1
                        dve.wait_ge(turned, flips[0])
                        step(dve.tensor_copy(kin[:], ptk[:]))
                        step(dve.tensor_copy(pin[:], ptp[:]))
                        layout = need
                    if j == k - 1:
                        if k > 8:
                            descending(k - 1, kin, layout)
                        descending(k, kin, layout)
                    d = 1 << (j if layout == "T" else j - 7)
                    pair = lambda a: a[:].rearrange("p (n two d) -> p n two d", two=2, d=d)
                    a, b = pair(kin)[:, :, 0, :], pair(kin)[:, :, 1, :]
                    m = swap[:].rearrange("p (n d) -> p n d", d=d)
                    dve.sem_inc(keys_ready, 1)
                    step(dve.tensor_tensor(m, a, b, ALU.is_gt))
                    dve.tensor_tensor(pair(kout)[:, :, 0, :], a, b, ALU.min)
                    step(dve.tensor_tensor(pair(kout)[:, :, 1, :], a, b, ALU.max))
                    dve.wait_ge(pay_copied, n + 1)
                    dve.copy_predicated(pair(pout)[:, :, 0, :], m, pair(pin)[:, :, 1, :])
                    step(dve.copy_predicated(pair(pout)[:, :, 1, :], m, pair(pin)[:, :, 0, :]))
                    if j == 0 and k < 8:
                        descending(k, kout, layout)

                dve.wait_ge(stored, 32)
                step(dve.tensor_copy(flat(cur), key[n_stage % 2][:]))
                dve.sem_inc(to_store, 1)
                dve.wait_ge(keys_back, 32)
                step(dve.tensor_tensor(flat(start), flat(cur), flat(oth), ALU.not_equal))
                step(dve.tensor_scalar(flat(start), flat(start), FAR, None, ALU.mult))
                dve.sem_inc(to_store, 1)
                spare = key[(n_stage + 1) % 2]
                step(dve.tensor_tensor(spare[:], flat(cur), flat(nrm), ALU.not_equal))
                step(dve.tensor_scalar(spare[:], spare[:], -float(SKIP), float(SKIP), ALU.mult, ALU.add))
                step(dve.tensor_tensor(spare[:], spare[:], flat(cur), ALU.add))
                step(dve.tensor_scalar(flat(oth), pay[n_stage % 2][:], E - 0.5, None, ALU.is_lt))
                step(dve.tensor_tensor(flat(oth), pay[n_stage % 2][:], flat(oth), ALU.mult))
                to_columns(spare[:], c.scat_s[:])
                to_columns(oth[:].rearrange("p b f -> p (b f)"), c.perm[:])

            @block.tensor
            def _(pe):
                n = 0

                def flip(psum, rows):
                    for b in range(NBLK):
                        ins = pe.transpose(psum[:, b * P:(b + 1) * P], rows[:, b * P:(b + 1) * P], ident[:])
                    return ins

                for _ in range(4 + c.NREL):
                    n += 1
                    pe.wait_ge(last_pay, n)
                    flip(ptk, pay[1]).then_inc(turned, 1)
                layout = "T"
                for m, (k, j) in enumerate(levels):
                    need = "T" if j < 7 else "A"
                    if need != layout:
                        n += 1
                        pe.wait_ge(last_pay, n)
                        flip(ptk, key[m % 2])
                        flip(ptp, pay[m % 2]).then_inc(turned, 1)
                        layout = need
                for _ in range(2):
                    n += 1
                    pe.wait_ge(last_pay, n)
                    flip(ptk, pay[1]).then_inc(turned, 1)


def setup(nc, c, w):
    sc = c.scope
    c.w_val0 = sc.sb("w_val0", [D, D])
    c.w_att0 = sc.sb("w_att0", [P, P])
    c.bias0 = sc.sb("bias0", [P, D])
    c.w_lr = sc.sb("w_lr", [P, D])
    c.w_e1 = sc.sb("w_e1", [16, D])
    c.b_g1 = sc.sb("b_g1", [D, 1])
    c.b_l1 = sc.sb("b_l1", [D, 1])
    c.w_att1 = sc.sb("w_att1", [D, P])
    c.bias1 = sc.sb("bias1", [P, D])
    c.gamma1, c.beta1 = sc.sb("gamma1", [P, D]), sc.sb("beta1", [P, D])
    c.w_qkv = sc.sb("w_qkv", [P, P])
    c.w_rpe = sc.sb("w_rpe", [19, P])
    c.w_head = sc.sb("w_head", [D + 4, P])
    c.w_rel01, c.w_rel2 = sc.sb("w_rel01", [P, D]), sc.sb("w_rel2", [D, D])
    c.w_gate = sc.sb("w_gate", [P, 4 * D])
    c.b_gate = sc.sb("b_gate", [1, 4 * D])
    c.gamma3, c.beta3 = sc.sb("gamma3", [P, D]), sc.sb("beta3", [P, D])
    c.scale1, c.shift1, c.scale3, c.shift3 = (sc.sb(n, [P, D]) for n in ("scale1", "shift1", "scale3", "shift3"))
    c.zero_col = sc.sb("zero_col", [P, 1])
    c.ones_row = sc.sb("ones_row", [1, P])
    scale = float(8) ** -0.5
    with Scope(nc, "setup") as s:
        wt = s.sb("wt", [D, 2, D])
        att_s, att_d = s.sb("att_s", [D, 1]), s.sb("att_d", [D, 1])
        att_w = s.sb("att_w", [D, 2, P])
        att1 = s.sb("att1", [D, 1])
        b_r = s.sb("b_r", [D, 1])
        brow = s.sb("brow", [1, 2, P])
        grow = s.sb("grow", [1, 2, 3 * D])
        gates = s.sb("gates", [D, 3, P])
        pa, pb, pc, pg = s.ps("pa"), s.ps("pb"), s.ps("pc"), s.ps("pg")
        filled, loaded, step_s, trans, prods, ready = (s.sem(n) for n in ("filled", "loaded", "step", "trans", "prods", "ready"))
        loads = []
        with nc.Block() as block:
            @block.gpsimd
            def _(pool):
                pool.memset(c.ident[:], 0.0).then_inc(filled, 1)
                pool.memset(c.w_qkv[:], 0.0).then_inc(filled, 1)
                pool.memset(c.w_gate[:], 0.0).then_inc(filled, 1)
                pool.memset(c.w_head[:], 1.0).then_inc(filled, 1)
                pool.memset(c.w_att1[:], 1.0).then_inc(filled, 1)
                pool.memset(c.ones_row[:], 1.0).then_inc(filled, 1)
                pool.memset(c.minus1[:], -1.0).then_inc(filled, 1)
                pool.memset(c.eps[:], LN_EPS).then_inc(filled, 1)
                pool.memset(c.zero_col[:], 0.0).then_inc(filled, 1)
                pool.wait_ge(filled, 9)
                pool.affine_select(out=c.ident[:], in_=c.ident[:], compare_op=ALU.not_equal, fill=1.0, base=0,
                                   pattern=[[-1, P]], channel_multiplier=1).then_inc(filled, 1)
                v = c.w_head[:].rearrange("p (a h f) -> p a h f", a=2, h=4)
                pool.affine_select(out=v, in_=v, compare_op=ALU.is_equal, fill=0.0, base=-D,
                                   pattern=[[0, 2], [-1, 4], [0, 16]], channel_multiplier=1).then_inc(filled, 1)
                v = c.w_att1[:].rearrange("p (a h f) -> p a h f", a=2, h=4)
                pool.affine_select(out=v, in_=v, compare_op=ALU.is_ge, fill=0.0, base=0,
                                   pattern=[[0, 2], [-16, 4], [0, 16]], channel_multiplier=1).then_inc(filled, 1)
                pool.wait_ge(filled, 12)
                pool.affine_select(out=v, in_=v, compare_op=ALU.is_ge, fill=0.0, base=15,
                                   pattern=[[0, 2], [16, 4], [0, 16]], channel_multiplier=-1).then_inc(filled, 1)

            @block.sync
            def _(sp):
                sp.wait_ge(filled, 9)
                n = [0]

                def ld(out, in_):
                    sp.dma_start(out, in_).then_inc(loaded, 16)
                    n[0] += 1

                col = lambda v: v.rearrange("(p a) -> p a", a=1)
                row = lambda v: v.rearrange("(a p) -> a p", a=1)
                wide = lambda v: row(v).to_broadcast([P, D])
                ld(c.w_val0[:], w["L0_gnn_W"])
                ld(att_s[:], col(w["L0_gnn_att_src"]))
                ld(att_d[:], col(w["L0_gnn_att_dst"]))
                ld(c.bias0[:], wide(w["L0_gnn_bias"]))
                ld(c.w_lr[0:D, :], w["L1_gnn_W_l"])
                ld(c.w_lr[D:P, :], w["L1_gnn_W_r"])
                ld(c.w_e1[:], w["L1_gnn_W_e"])
                ld(c.b_l1[:], col(w["L1_gnn_b_l"]))
                ld(b_r[:], col(w["L1_gnn_b_r"]))
                ld(att1[:], w["L1_gnn_att"].rearrange("h (c a) -> (h c) a", a=1))
                ld(c.bias1[:], wide(w["L1_gnn_bias"]))
                ld(c.gamma1[:], wide(w["L1_gnn_gamma"]))
                ld(c.beta1[:], wide(w["L1_gnn_beta"]))
                ld(c.w_qkv[0:D, 0:32], w["L2_gnn_qkv_w"][:, 0:32])
                ld(c.w_qkv[D:P, 32:P], w["L2_gnn_qkv_w"][:, 32:P])
                ld(c.w_rpe[1:19, 0:32], w["L2_gnn_q_rpe_w"])
                ld(c.w_rpe[1:19, 32:64], w["L2_gnn_k_rpe_w"])
                ld(c.w_rpe[1:19, 64:128], w["L2_gnn_v_rpe_w"])
                ld(brow[:, 0, :], row(w["L2_gnn_qkv_b"]))
                ld(brow[:, 1, 0:32], row(w["L2_gnn_q_rpe_b"]))
                ld(brow[:, 1, 32:64], row(w["L2_gnn_k_rpe_b"]))
                ld(brow[:, 1, 64:128], row(w["L2_gnn_v_rpe_b"]))
                ld(c.w_rel01[0:D, :], w["L3_gnn_weight"][0])
                ld(c.w_rel01[D:P, :], w["L3_gnn_weight"][1])
                ld(c.w_rel2[:], w["L3_gnn_weight"][2])
                ld(gates[:, :, 0:D], w["L3_gnn_w_ih"].rearrange("(g p) f -> p g f", g=3))
                ld(gates[:, :, D:P], w["L3_gnn_w_hh"].rearrange("(g p) f -> p g f", g=3))
                ld(grow[:, 0, :], row(w["L3_gnn_b_ih"]))
                ld(grow[:, 1, :], row(w["L3_gnn_b_hh"]))
                ld(c.gamma3[:], wide(w["L3_gnn_gamma"]))
                ld(c.beta3[:], wide(w["L3_gnn_beta"]))
                loads.append(n[0])

            @block.vector
            def _(dve):
                step = Chain(dve, step_s)
                dve.wait_ge(filled, 13)
                dve.wait_ge(loaded, 16 * loads[0])
                step(dve.tensor_copy(att_w[:, 0, :], att_s[:, 0:1].to_broadcast([D, P])))
                step(dve.tensor_copy(att_w[:, 1, :], att_d[:, 0:1].to_broadcast([D, P])))
                step(dve.tensor_tensor(c.b_g1[:], c.b_l1[:], b_r[:], ALU.add))
                step(dve.tensor_scalar(c.w_att1[:], c.w_att1[:], att1[:, 0:1], None, ALU.mult))
                step(dve.tensor_scalar(c.w_qkv[0:D, 0:32], c.w_qkv[0:D, 0:32], scale, None, ALU.mult))
                step(dve.tensor_scalar(brow[:, 0, 0:32], brow[:, 0, 0:32], scale, None, ALU.mult))
                step(dve.tensor_tensor(c.w_rpe[0:1, :], brow[:, 0, :], brow[:, 1, :], ALU.add))
                step(dve.tensor_tensor(c.b_gate[:, 0:2 * D], grow[:, 0, 0:2 * D], grow[:, 1, 0:2 * D], ALU.add))
                step(dve.tensor_copy(c.b_gate[:, 2 * D:3 * D], grow[:, 0, 2 * D:3 * D]))
                step(dve.tensor_copy(c.b_gate[:, 3 * D:4 * D], grow[:, 1, 2 * D:3 * D]))
                dve.wait_ge(trans, 1)
                step(dve.tensor_copy(wt[:, 0, :], pa[0:D, 0:D]))
                step(dve.tensor_copy(wt[:, 1, :], pa[0:D, 0:D]))
                step(dve.tensor_copy(c.w_gate[:, 0:2 * D], pg[:, 0:2 * D]))
                step(dve.tensor_copy(c.w_gate[0:D, 2 * D:3 * D], pg[0:D, 2 * D:3 * D]))
                step(dve.tensor_copy(c.w_gate[D:P, 3 * D:4 * D], pg[D:P, 2 * D:3 * D]))
                dve.sem_inc(ready, 1)
                dve.wait_ge(prods, 1)
                step(dve.tensor_copy(c.w_att0[0:D, :], pb[0:D, 0:P]))
                step(dve.tensor_copy(c.w_att0[D:P, :], pc[D:P, 0:P]))

            @block.tensor
            def _(pe):
                pe.wait_ge(filled, 13)
                pe.wait_ge(loaded, 16 * loads[0])
                pe.transpose(pa[0:D, 0:D], c.w_val0[:], c.ident[0:D, 0:D])
                for g in range(3):
                    ins = pe.transpose(pg[:, g * D:(g + 1) * D], gates[:, g, :], c.ident[0:D, 0:D])
                ins.then_inc(trans, 1)
                pe.wait_ge(ready, 1)
                both = wt[:].rearrange("p a f -> p (a f)")
                pe.matmul(pb[:, 0:P], both, att_w[:, 0, :], start=True, stop=True)
                pe.matmul(pc[:, 0:P], both, att_w[:, 1, :], start=True, stop=True).then_inc(prods, 1)


def rows4(v):
    return v.unsqueeze(2).to_broadcast([v.shape[0], v.shape[1], D])


def over_rows(v, n):
    return v.unsqueeze(1).to_broadcast([v.shape[0], n, v.shape[1]])


class Norm:

    def __init__(self, s, name, R):
        self.R = R
        self.mean, self.var, self.lnv, self.rstd = (s.sb(f"{name}_{n}", [P, R]) for n in ("mean", "var", "lnv", "rstd"))
        self.cen = s.sb(f"{name}_cen", [P, R, D])
        self.sq = s.sb(f"{name}_sq", [P, R, D])
        self.centered, self.squared, self.summed, self.scaled = (s.sem(f"{name}_{n}") for n in ("centered", "squared", "summed", "scaled"))

    def vector(self, dve, step, n, x, outs, p=P):
        R = self.R
        step(dve.tensor_reduce(self.mean[0:p, :], x, AX, ALU.add))
        step(dve.scalar_tensor_tensor(self.cen[0:p], rows4(self.mean[0:p, :]), -1.0 / D, x, ALU.mult, ALU.add))
        dve.sem_inc(self.centered, 1)
        dve.wait_ge(self.squared, n)
        step(dve.tensor_reduce(self.var[0:p, :], self.sq[0:p], AX, ALU.add))
        dve.sem_inc(self.summed, 1)
        dve.wait_ge(self.scaled, n)
        for out, factor in outs:
            r = self.rstd[0:p, :]
            if factor is not None:
                step(dve.tensor_tensor(self.var[0:p, :], r, factor, ALU.mult))
                r = self.var[0:p, :]
            step(dve.scalar_tensor_tensor(out, self.cen[0:p], 0.0, rows4(r), ALU.max, ALU.mult))

    def scalar(self, act, step, n, eps, p=P):
        act.wait_ge(self.centered, n)
        act.activation(self.sq[0:p], self.cen[0:p], ACT.Square).then_inc(self.squared, 1)
        act.wait_ge(self.summed, n)
        step(act.activation(self.lnv[0:p, :], self.var[0:p, :], ACT.Ln, bias=eps[0:p, 0:1], scale=1.0 / D))
        act.activation(self.rstd[0:p, :], self.lnv[0:p, :], ACT.Exp, scale=-0.5).then_inc(self.scaled, 1)


class Softmax:

    def __init__(self, s):
        self.far = [s.sb(f"far{u}", [P, CE]) for u in range(2)]
        self.score = s.sb("score", [P, CE])
        self.top = [s.sb(f"top{u}", [P, CE + 1]) for u in range(2)]
        self.ex = s.sb("ex", [P, 2, CE])
        self.sums = [s.sb(f"sums{u}", [P, CE]) for u in range(2)]
        self.den = s.sb("den", [P, TPC, D])
        self.res = s.sb("res", [P, TPC, D])
        self.p_sums = s.ps("p_sums")
        self.far_loaded = [s.sem(f"far_loaded{u}") for u in range(2)]
        self.far_used, self.shifted, self.exped, self.summed, self.sums_turned, self.sums_taken = (
            s.sem(n) for n in ("far_used", "shifted", "exped", "run_summed", "sums_turned", "sums_taken"))

    def load(self, sp, i, t, u, first, row, n):
        if not first:
            sp.wait_ge(self.far_used, n - 2)
        sp.dma_start(self.far[u][:], row[bass.ds(i * CE, CE)].rearrange("(a f) -> a f", a=1).to_broadcast([P, CE])
                     ).then_inc(self.far_loaded[u], 16)

    def vector(self, dve, step, n, t, u, start, weigh):
        top, far = self.top[u], self.far[u]
        if start:
            step(dve.memset(top[:, 0:1], FAR))
        else:
            step(dve.tensor_copy(top[:, 0:1], self.top[1 - u][:, CE:CE + 1]))
        dve.wait_ge(self.far_loaded[u], 16 * (t + 1))
        step(dve.tensor_tensor_scan(top[:, 1:CE + 1], far[:], self.score[:], top[:, 0:1], ALU.add, ALU.max))
        step(dve.tensor_tensor(self.ex[:, 0, :], top[:, 0:CE], far[:], ALU.add))
        dve.sem_inc(self.far_used, 1)
        step(dve.tensor_tensor(self.ex[:, 0, :], self.ex[:, 0, :], top[:, 1:CE + 1], ALU.subtract))
        step(dve.tensor_tensor(self.ex[:, 1, :], self.score[:], top[:, 1:CE + 1], ALU.subtract))
        dve.sem_inc(self.shifted, 1)
        dve.wait_ge(self.exped, n)
        step(weigh(self.ex[0:D, 1, :]))
        step(dve.tensor_tensor_scan(self.sums[u][:], self.ex[:, 0, :], self.ex[:, 1, :],
                                    0.0 if start else self.sums[1 - u][:, CE - 1:CE], ALU.mult, ALU.add))
        dve.sem_inc(self.summed, 1)
        dve.wait_ge(self.sums_turned, n)
        v = self.p_sums[:].rearrange("p (j f) -> p j f", j=TPC)
        step(dve.tensor_scalar(self.den[:], v[:, :, D:P], 1e-16, None, ALU.add))
        step(dve.reciprocal(self.den[:], self.den[:]))
        step(dve.tensor_tensor(self.res[:], v[:, :, 0:D], self.den[:], ALU.mult))
        dve.sem_inc(self.sums_taken, 1)

    def scalar(self, act, n):
        act.wait_ge(self.shifted, n)
        act.activation(self.ex[:], self.ex[:], ACT.Exp).then_inc(self.exped, 1)

    def tensor(self, pe, c, n, u, first):
        pe.wait_ge(self.summed, n)
        if not first:
            pe.wait_ge(self.sums_taken, n - 1)
        for j in range(TPC):
            ins = pe.transpose(self.p_sums[:, j * P:(j + 1) * P], self.sums[u][:, j * P:(j + 1) * P], c.ident[:])
        ins.then_inc(self.sums_turned, 1)


class Rows:

    def __init__(self, s, lists, width):
        self.lists = lists
        self.buf = [s.sb(f"rows{u}", [P, TPC, width]) for u in range(2)]
        self.num = [s.sb(f"num{u}", [P, len(lists), TPC], I32) for u in range(2)]
        self.gathered = [s.swdge_sem(f"gathered{u}") for u in range(2)]
        self.num_ready = s.sem("num_ready")
        self.rows_free = s.sem("rows_free")
        self.per = 16 * TPC * len(lists)

    def gather(self, pool, i, t, u, n, first):
        if not first:
            hold(pool, self.rows_free, n - 2)
        for k, (_, _, _, lst) in enumerate(self.lists):
            pool.tensor_copy(self.num[u][:, k, :], lst[:, bass.ds(i * TPC, TPC)]).then_inc(self.num_ready, 1)
        hold(pool, self.num_ready, n * len(self.lists))
        for k, (table, w, at, _) in enumerate(self.lists):
            for j in range(TPC):
                pool.indirect_dma_start(self.buf[u][:, j, at:at + w], None, table,
                                        bass.IndirectOffsetOnAxis(ap=self.num[u][:, k, j:j + 1], axis=0)
                                        ).then_inc(self.gathered[u], 16)


class Scatter:
    def __init__(self, s, table, width, lst, rows):
        self.table, self.lst, self.rows = table, lst, rows
        self.num = [s.sb(f"snum{u}", [P, TPC], I32) for u in range(2)]
        self.out = [s.sb(f"out{u}", [P, TPC, width]) for u in range(2)]
        self.scattered = [s.swdge_sem(f"scattered{u}") for u in range(2)]
        self.snum_ready, self.out_ready = s.sem("snum_ready"), s.sem("out_ready")

    def scatter(self, pool, i, t, u, n, first):
        if not first:
            hold(pool, self.scattered[u], 16 * TPC * t)
        pool.tensor_copy(self.num[u][:], self.lst[:, bass.ds(i * TPC, TPC)]).then_inc(self.snum_ready, 1)
        pool.wait_ge(self.snum_ready, n)
        hold(pool, self.out_ready, n)
        for j in range(TPC):
            pool.indirect_dma_start(self.table, bass.IndirectOffsetOnAxis(ap=self.num[u][:, j:j + 1], axis=0),
                                    self.out[u][:, j, :], None, bounds_check=self.rows - 1, oob_is_err=False
                                    ).then_inc(self.scattered[u], 16)

    def free(self, eng, t, u, first):
        if not first:
            eng.wait_ge(self.scattered[u], 16 * TPC * t)

    def done(self, eng, turns_):
        for u in range(2):
            eng.wait_ge(self.scattered[u], 16 * TPC * turns_)


def chunks(eng, n_turns, body):
    def turn(t, a, b):
        for u in range(2):
            body(2 * t + u, t, u, 2 * t + u + 1, a, b and u == 1)
    turns(eng, n_turns, turn)


def pool_program(pool, rows, sct, n_turns):
    rows.gather(pool, 0, 0, 0, 1, True)

    def turn(t, a, b):
        rows.gather(pool, 2 * t + 1, t, 1, 2 * t + 2, a)
        if sct:
            sct.scatter(pool, 2 * t, t, 0, 2 * t + 1, a)
        if not b:
            rows.gather(pool, 2 * t + 2, t + 1, 0, 2 * t + 3, False)
        if sct:
            sct.scatter(pool, 2 * t + 1, t, 1, 2 * t + 2, a)
    turns(pool, n_turns, turn)
    if sct:
        sct.done(pool, n_turns)


def node_rows(table, ch, parts, width):
    return table[bass.ds(ch * (P * NR), parts * NR), :].rearrange("(p r) f -> p r f", r=NR)


def node_chunks(eng, c, body):
    rest = (c.N - (c.NCH - 1) * P * NR) // NR
    assert (c.N - (c.NCH - 1) * P * NR) % NR == 0 and 0 < rest <= P

    def one(i, t, u, n, first, last):
        body(i, t, u, n, first, rest if last else P)
    chunks(eng, c.TURNS, one)


def dense_start(nc, c, x, tab1, tab2):
    with Scope(nc, "ds") as s:
        xin = [s.sb(f"xin{u}", [P, NR, D]) for u in range(2)]
        row = [s.sb(f"row{u}", [P, NR, P]) for u in range(2)]
        tb = s.sb("tb", [P, D])
        xin_loaded = [s.sem(f"xin_loaded{u}") for u in range(2)]
        stored = [s.sem(f"stored{u}") for u in range(2)]
        row_done, tanh_done = s.sem("row_done"), s.sem("tanh_done")
        with nc.Block() as block:
            @block.scalar
            def _(act):
                act.activation(tb[:], c.bias0[:], ACT.Tanh).then_inc(tanh_done, 1)

            @block.sync
            def _(sp):
                def store(i, t, u, n, parts):
                    sp.wait_ge(row_done, n)
                    sp.dma_start(node_rows(tab1, i, parts, D), row[u][0:parts, :, 0:D]).then_inc(stored[u], 16)
                    sp.dma_start(node_rows(tab2, i, parts, P), row[u][0:parts]).then_inc(stored[u], 16)

                def body(i, t, u, n, first, parts):
                    if not first:
                        sp.wait_ge(row_done, n - 2)
                    sp.dma_start(xin[u][0:parts], node_rows(x, i, parts, D)).then_inc(xin_loaded[u], 16)
                    if not (first and u == 0):
                        store(*prev(i, t, u, n), P)

                def prev(i, t, u, n):
                    return (i - 1, t, 0, n - 1) if u else (i - 1, t - 1, 1, n - 1)
                node_chunks(sp, c, body)
                rest = (c.N - (c.NCH - 1) * P * NR) // NR
                store(c.NCH - 1, c.TURNS - 1, 1, c.NCH, rest)
                for u in range(2):
                    sp.wait_ge(stored[u], 32 * c.TURNS)

            @block.vector
            def _(dve):
                dve.wait_ge(tanh_done, 1)
                for u in range(2):
                    dve.tensor_copy(row[u][:, :, D:P], over_rows(c.bias1[:], NR))

                def body(i, t, u, n, first, parts):
                    dve.wait_ge(xin_loaded[u], 16 * (t + 1))
                    if not first:
                        dve.wait_ge(stored[u], 32 * t)
                    dve.tensor_tensor(row[u][0:parts, :, 0:D], xin[u][0:parts], over_rows(tb[0:parts, :], NR), ALU.add).then_inc(row_done, 1)
                node_chunks(dve, c, body)


def fill_rows(nc, c, name, table, row):
    with Scope(nc, name) as s:
        tile_ = s.sb("tile", [P, NR, D])
        made, stored = s.sem("made"), s.sem("stored")
        with nc.Block() as block:
            @block.vector
            def _(dve):
                dve.tensor_copy(tile_[:], over_rows(row, NR)).then_inc(made, 1)

            @block.sync
            def _(sp):
                sp.wait_ge(made, 1)

                def body(i, t, u, n, first, parts):
                    sp.dma_start(node_rows(table, i, parts, D), tile_[0:parts]).then_inc(stored, 16)
                node_chunks(sp, c, body)
                sp.wait_ge(stored, 16 * c.NCH)


def conv_gat(nc, c, x, dram, tab1):
    with Scope(nc, "l0") as s:
        rows = Rows(s, [(x, D, 0, c.idx_src), (x, D, D, c.idx_dst)], 2 * D)
        sct = Scatter(s, tab1, D, c.scat_d, c.N)
        norm = Norm(s, "n", 2 * TPC)
        sm = Softmax(s)
        h = s.sb("h", [P, TPC, 2 * D])
        hT = s.sb("hT", [P, CE])
        leak = s.sb("leak", [P, CE])
        e2 = s.sb("e2", [P, TPC, D])
        p_hT, p_val, p_score = s.ps("p_hT"), s.ps("p_val", (D, CE)), s.ps("p_score")
        m = s.sems("h_ready h_turned hT_ready scored leaked out_ready2 exp2 dve_step act_step scores_taken")
        with nc.Block() as block:
            @block.sync
            def _(sp):
                def body(i, t, u, n, first, last):
                    sm.load(sp, i, t, u, first, dram["far_d"], n)
                chunks(sp, c.TURNS, body)

            @block.gpsimd
            def _(pool):
                pool_program(pool, rows, sct, c.TURNS)

            @block.scalar
            def _(act):
                step = Chain(act, m["act_step"])

                def body(i, t, u, n, first, last):
                    if u == 0:
                        step.restart(first)
                    norm.scalar(act, step, n, c.eps)
                    act.wait_ge(m["h_turned"], n)
                    act.activation(hT[:], p_hT[:], ACT.Copy).then_inc(m["hT_ready"], 1)
                    act.wait_ge(m["scored"], n)
                    act.activation(leak[:], p_score[:], ACT.Copy, scale=0.2).then_inc(m["leaked"], 1)
                    sm.scalar(act, n)
                    act.wait_ge(m["out_ready2"], n)
                    act.activation(e2[:], sm.res[:], ACT.Exp, scale=2.0).then_inc(m["exp2"], 1)
                chunks(act, c.TURNS, body)

            @block.vector
            def _(dve):
                step = Chain(dve, m["dve_step"])

                def body(i, t, u, n, first, last):
                    if u == 0:
                        step.restart(first)
                    buf = rows.buf[u]
                    dve.wait_ge(rows.gathered[u], rows.per * (t + 1))
                    norm.vector(dve, step, n, buf[:].rearrange("p j (a f) -> p (j a) f", f=D),
                                [(h[:].rearrange("p j (a f) -> p (j a) f", f=D), None)])
                    dve.sem_inc(m["h_ready"], 1)
                    dve.wait_ge(m["leaked"], n)
                    step(dve.tensor_tensor(sm.score[:], p_score[:], leak[:], ALU.max))
                    dve.sem_inc(m["scores_taken"], 1)
                    sm.vector(dve, step, n, t, u, first and u == 0,
                              lambda p_: dve.tensor_tensor(p_, p_, p_val[:], ALU.mult))
                    step(dve.tensor_tensor(sm.res[:], sm.res[:], over_rows(c.bias0[:], TPC), ALU.add))
                    dve.sem_inc(m["out_ready2"], 1)
                    dve.wait_ge(m["exp2"], n)
                    step(dve.tensor_scalar(e2[:], e2[:], 1.0, None, ALU.add))
                    step(dve.reciprocal(e2[:], e2[:]))
                    step(dve.tensor_scalar(e2[:], e2[:], -2.0, 1.0, ALU.mult, ALU.add))
                    sct.free(dve, t, u, first)
                    step(dve.tensor_tensor(sct.out[u][:], e2[:], buf[:, :, D:2 * D], ALU.add))
                    dve.sem_inc(sct.out_ready, 1)
                    dve.sem_inc(rows.rows_free, 1)
                chunks(dve, c.TURNS, body)

            @block.tensor
            def _(pe):
                def body(i, t, u, n, first, last):
                    pe.wait_ge(m["h_ready"], n)
                    for j in range(TPC):
                        ins = pe.transpose(p_hT[:, j * P:(j + 1) * P], h[:, j, :], c.ident[:])
                    ins.then_inc(m["h_turned"], 1)
                    hold(pe, m["hT_ready"], n)
                    pe.matmul(p_val[:], c.w_val0[:], hT[0:D, :], start=True, stop=True)
                    pe.matmul(p_score[:], c.w_att0[:], hT[:], start=True, stop=True).then_inc(m["scored"], 1)
                    sm.tensor(pe, c, n, u, first and u == 0)
                chunks(pe, c.TURNS, body)


def conv_gatv2(nc, c, dram, x1, x1o, edge_attr):
    with Scope(nc, "l1") as s:
        rows = Rows(s, [(x1, D, 0, c.idx_src), (x1, D, D, c.idx_dst)], 2 * D)
        sct = Scatter(s, x1o, 2 * D, c.scat_d, c.N)
        norm = Norm(s, "n", 2 * TPC)
        sm = Softmax(s)
        h = s.sb("h", [P, TPC, 2 * D])
        hT = s.sb("hT", [P, CE])
        ea = EdgeAttr(s, edge_attr, 16, 0)
        g = s.sb("g", [D, CE])
        sums = s.sb("sums", [P, TPC, 2 * D])
        last = s.sb("last", [P, TPC])
        stat = Stats(s)
        p_hT, p_g, p_val, p_score = s.ps("p_hT"), s.ps("p_g", (D, CE)), s.ps("p_val", (D, CE)), s.ps("p_score")
        m = s.sems("h_ready h_turned hT_ready g_summed g_out g_ready scored scores_out dve_step act_step sums_ready sums_added")
        with nc.Block() as block:
            @block.sync
            def _(sp):
                def body(i, t, u, n, first, last_):
                    sm.load(sp, i, t, u, first, dram["far_d"], n)
                    ea.load(sp, c, i, t, u, n, first, last_)
                chunks(sp, c.TURNS, body)

            @block.gpsimd
            def _(pool):
                ea.clear(pool)
                pool_program(pool, rows, sct, c.TURNS)

            @block.scalar
            def _(act):
                step = Chain(act, m["act_step"])

                def body(i, t, u, n, first, last_):
                    if u == 0:
                        step.restart(first)
                    ea.scalar(act, n)
                    norm.scalar(act, step, n, c.eps)
                    act.wait_ge(m["h_turned"], n)
                    act.activation(hT[:], p_hT[:], ACT.Copy).then_inc(m["hT_ready"], 1)
                    act.wait_ge(m["g_summed"], n)
                    act.activation(g[:], p_g[:], ACT.Identity, bias=c.b_g1[:, 0:1]).then_inc(m["g_out"], 1)
                    act.wait_ge(m["scored"], n)
                    act.activation(sm.score[:], p_score[:], ACT.Copy).then_inc(m["scores_out"], 1)
                    sm.scalar(act, n)
                chunks(act, c.TURNS, body)
                stat.scalar(act, c)

            @block.vector
            def _(dve):
                step = Chain(dve, m["dve_step"])

                def body(i, t, u, n, first, last_):
                    if u == 0:
                        step.restart(first)
                    buf = rows.buf[u]
                    dve.wait_ge(rows.gathered[u], rows.per * (t + 1))
                    norm.vector(dve, step, n, buf[:].rearrange("p j (a f) -> p (j a) f", f=D),
                                [(h[:].rearrange("p j (a f) -> p (j a) f", f=D), None)])
                    dve.sem_inc(m["h_ready"], 1)
                    dve.wait_ge(m["g_out"], n)
                    step(dve.scalar_tensor_tensor(g[:], g[:], 0.2, g[:], ALU.mult, ALU.max))
                    dve.sem_inc(m["g_ready"], 1)
                    dve.wait_ge(m["scores_out"], n)
                    sm.vector(dve, step, n, t, u, first and u == 0,
                              lambda p_: dve.scalar_tensor_tensor(p_, p_val[:], c.b_l1[:, 0:1], p_, ALU.add, ALU.mult))
                    sct.free(dve, t, u, first)
                    if not (first and u == 0):
                        dve.wait_ge(m["sums_added"], n - 1)
                    step(dve.tensor_copy(last[:], c.last_d[:, bass.ds(i * TPC, TPC)]))
                    step(dve.tensor_copy(sums[:, :, 0:D], sm.res[:]))
                    step(dve.tensor_tensor(sums[:, :, D:P], sm.res[:], sm.res[:], ALU.mult))
                    dve.sem_inc(m["sums_ready"], 1)
                    step(dve.tensor_copy(sct.out[u][:, :, 0:D], buf[:, :, D:2 * D]))
                    step(dve.tensor_tensor(sct.out[u][:, :, D:P], sm.res[:], over_rows(c.bias1[:], TPC), ALU.add))
                    dve.sem_inc(sct.out_ready, 1)
                    dve.sem_inc(rows.rows_free, 1)
                chunks(dve, c.TURNS, body)
                stat.vector(dve, Chain(dve, stat.step), c, c.gamma1, c.beta1, c.bias1, c.scale1, c.shift1)

            @block.tensor
            def _(pe):
                stat.begin(pe, c)

                def body(i, t, u, n, first, last_):
                    ea.tensor(pe, c, n, t, u, first and u == 0)
                    pe.wait_ge(m["h_ready"], n)
                    for j in range(TPC):
                        ins = pe.transpose(p_hT[:, j * P:(j + 1) * P], h[:, j, :], c.ident[:])
                    ins.then_inc(m["h_turned"], 1)
                    hold(pe, m["hT_ready"], n)
                    hold(pe, ea.ready, n)
                    pe.matmul(p_g[:], c.w_lr[:], hT[:], start=True, stop=False)
                    pe.matmul(p_g[:], c.w_e1[:], ea.T[0:16, :], start=False, stop=True).then_inc(m["g_summed"], 1)
                    pe.matmul(p_val[:], c.w_lr[0:D, :], hT[0:D, :], start=True, stop=True)
                    hold(pe, m["g_ready"], n)
                    pe.matmul(p_score[:], c.w_att1[:], g[:], start=True, stop=True).then_inc(m["scored"], 1)
                    sm.tensor(pe, c, n, u, first and u == 0)
                    hold(pe, m["sums_ready"], n)
                    stat.add(pe, last, sums, m["sums_added"])
                chunks(pe, c.TURNS, body)
                stat.finish(pe, c)


class EdgeAttr:

    def __init__(self, s, table, width, ones):
        self.table, self.w, self.ones = table, width, ones
        self.rows = [s.sb(f"ea{u}", [P, TPC, 32]) for u in range(2)]
        self.T = s.sb("eaT", [32, CE])
        self.p = s.ps("p_ea", (32, CE))
        self.loaded = [s.sem(f"ea_loaded{u}") for u in range(2)]
        self.turned, self.ready, self.cleared, self.used = s.sem("ea_turned"), s.sem("ea_ready"), s.sem("ea_cleared"), s.sem("ea_used")

    def clear(self, pool):
        for u in range(2):
            pool.memset(self.rows[u][:], 1.0).then_inc(self.cleared, 1)

    def load(self, sp, c, i, t, u, n, first, last):
        if first:
            sp.wait_ge(self.cleared, 2)
        else:
            sp.wait_ge(self.turned, n - 2)
        o = self.ones
        if not last:
            sp.dma_start(self.rows[u][:, :, o:o + self.w],
                         self.table[bass.ds(i * CE, CE), :].rearrange("(j p) f -> p j f", p=P)).then_inc(self.loaded[u], 16)
            return
        base = (c.NCH - 1) * CE
        tiles, rest = (c.E - base) // P, (c.E - base) % P
        sp.dma_start(self.rows[u][:, 0:tiles, o:o + self.w],
                     self.table[base:base + tiles * P, :].rearrange("(j p) f -> p j f", p=P)).then_inc(self.loaded[u], 16)
        sp.dma_start(self.rows[u][0:rest, tiles, o:o + self.w], self.table[base + tiles * P:c.E, :]).then_inc(self.loaded[u], 16)

    def tensor(self, pe, c, n, t, u, first):
        last = isinstance(t, int) and t == c.TURNS - 1 and u == 1
        hold(pe, self.loaded[u], 16 * (t + 1) + (16 if last else 0))
        if not first:
            hold(pe, self.ready, n - 1)
        for j in range(TPC):
            ins = pe.transpose(self.p[0:32, j * P:(j + 1) * P], self.rows[u][:, j, :], c.ident[:])
        ins.then_inc(self.turned, 1)

    def scalar(self, act, n, used=None):
        act.wait_ge(self.turned, n)
        if used is not None:
            act.wait_ge(*used)
        act.activation(self.T[:], self.p[:], ACT.Copy).then_inc(self.ready, 1)


class Stats:

    def __init__(self, s):
        self.p = s.ps("p_stat", (P, CE))
        self.row = s.sb("stat_row", [1, P])
        self.b = s.sb("stat_b", [P, P])
        self.step, self.zeroed, self.summed, self.row_out, self.spread = (s.sem("stat_" + n) for n in ("step", "zeroed", "summed", "row_out", "spread"))
        self.lnv = s.sb("stat_lnv", [P, D])
        self.var = s.sb("stat_var", [P, D])
        self.ln_done, self.var_done = s.sem("stat_ln_done"), s.sem("stat_var_done")

    def begin(self, pe, c):
        pe.matmul(self.p[0:1, 0:P], c.zero_col[:, 0:1], c.ident[:], start=True, stop=False, skip_group_check=True)

    def add(self, pe, last, sums, done):
        for j in range(TPC):
            ins = pe.matmul(self.p[0:1, 0:P], last[:, j:j + 1], sums[:, j, :], start=False, stop=False, skip_group_check=True)
        ins.then_inc(done, 1)

    def finish(self, pe, c):
        pe.matmul(self.p[0:1, 0:P], c.zero_col[:, 0:1], c.ident[:], start=False, stop=True, skip_group_check=True).then_inc(self.summed, 1)
        pe.wait_ge(self.row_out, 1)
        pe.matmul(self.p[:, 2 * P:3 * P], c.ones_row[:], self.row[:], start=True, stop=True).then_inc(self.spread, 1)

    def scalar(self, act, c):
        act.wait_ge(self.var_done, 1)
        act.activation(self.lnv[:], self.var[:], ACT.Ln, bias=c.eps[:, 0:1]).then_inc(self.ln_done, 1)
        act.wait_ge(self.ln_done, 1)
        act.activation(self.lnv[:], self.lnv[:], ACT.Exp, scale=-0.5).then_inc(self.ln_done, 1)

    def vector(self, dve, step, c, gamma, beta, offset, scale, shift):
        dve.wait_ge(self.summed, 1)
        step(dve.tensor_scalar(self.row[:], self.p[0:1, 0:P], 1.0 / c.N, None, ALU.mult))
        dve.sem_inc(self.row_out, 1)
        dve.wait_ge(self.spread, 1)
        step(dve.tensor_copy(self.b[:], self.p[:, 2 * P:3 * P]))
        mean, sq = self.b[:, 0:D], self.b[:, D:P]
        step(dve.tensor_tensor(self.lnv[:], mean, mean, ALU.mult))
        step(dve.tensor_tensor(self.var[:], sq, self.lnv[:], ALU.subtract))
        dve.sem_inc(self.var_done, 1)
        dve.wait_ge(self.ln_done, 2)
        step(dve.tensor_tensor(scale[:], self.lnv[:], gamma[:], ALU.mult))
        step(dve.tensor_tensor(mean, mean, offset[:], ALU.add))
        step(dve.tensor_tensor(mean, mean, scale[:], ALU.mult))
        step(dve.tensor_tensor(shift[:], beta[:], mean, ALU.subtract))


class Second:

    def __init__(self, s, R):
        self.R = R
        self.norm = Norm(s, "nx", R)
        self.y = s.sb("y", [P, R, D])
        self.x2 = s.sb("x2", [P, R, D])
        self.bn_ready, self.gelu_done = s.sem("bn_ready"), s.sem("gelu_done")

    def vector(self, dve, step, c, n, rows, p=P):
        R, y, x2 = self.R, self.y, self.x2
        self.norm.vector(dve, step, n, rows[:, :, 0:D], [(x2[0:p], None)], p)
        step(dve.tensor_tensor(y[0:p], rows[:, :, D:P], over_rows(c.scale1[0:p, :], R), ALU.mult))
        step(dve.tensor_tensor(x2[0:p], x2[0:p], over_rows(c.shift1[0:p, :], R), ALU.add))
        step(dve.tensor_tensor(y[0:p], y[0:p], x2[0:p], ALU.add))
        dve.sem_inc(self.bn_ready, 1)
        dve.wait_ge(self.gelu_done, n)
        step(dve.tensor_tensor(x2[0:p], y[0:p], rows[:, :, 0:D], ALU.add))

    def scalar(self, act, step, c, n, p=P):
        self.norm.scalar(act, step, n, c.eps, p)
        act.wait_ge(self.bn_ready, n)
        act.activation(self.y[0:p], self.y[0:p], ACT.Gelu).then_inc(self.gelu_done, 1)


def dense_second(nc, c, x1o, xd):
    with Scope(nc, "d2") as s:
        rin = [s.sb(f"rin{u}", [P, NR, P]) for u in range(2)]
        out = [s.sb(f"out{u}", [P, NR, D]) for u in range(2)]
        sec = Second(s, NR)
        loaded = [s.sem(f"loaded{u}") for u in range(2)]
        stored = [s.sem(f"stored{u}") for u in range(2)]
        done, dve_step, act_step = s.sem("done"), s.sem("dve_step"), s.sem("act_step")
        with nc.Block() as block:
            @block.sync
            def _(sp):
                def store(i, u, n, parts):
                    sp.wait_ge(done, n)
                    sp.dma_start(node_rows(xd, i, parts, D), out[u][0:parts]).then_inc(stored[u], 16)

                def body(i, t, u, n, first, parts):
                    if not first:
                        sp.wait_ge(done, n - 2)
                    sp.dma_start(rin[u][0:parts], node_rows(x1o, i, parts, P)).then_inc(loaded[u], 16)
                    if not (first and u == 0):
                        store(i - 1, 1 - u, n - 1, P)
                node_chunks(sp, c, body)
                store(c.NCH - 1, 1, c.NCH, (c.N - (c.NCH - 1) * P * NR) // NR)
                for u in range(2):
                    sp.wait_ge(stored[u], 16 * c.TURNS)

            @block.vector
            def _(dve):
                step = Chain(dve, dve_step)

                def body(i, t, u, n, first, parts):
                    if u == 0:
                        step.restart(first)
                    dve.wait_ge(loaded[u], 16 * (t + 1))
                    sec.vector(dve, step, c, n, rin[u][0:parts], parts)
                    if not first:
                        dve.wait_ge(stored[u], 16 * t)
                    step(dve.tensor_copy(out[u][0:parts], sec.x2[0:parts]))
                    dve.sem_inc(done, 1)
                node_chunks(dve, c, body)

            @block.scalar
            def _(act):
                step = Chain(act, act_step)

                def body(i, t, u, n, first, parts):
                    if u == 0:
                        step.restart(first)
                    sec.scalar(act, step, c, n, parts)
                node_chunks(act, c, body)


PAYW = 2 * D + 4


def edge_qkv(nc, c, x1o, pay, edge_attr):
    with Scope(nc, "l2") as s:
        rows = Rows(s, [(x1o, P, 0, c.idx_src), (x1o, P, P, c.idx_dst)], 4 * D)
        sec = Second(s, 2 * TPC)
        norm = Norm(s, "n", 2 * TPC)
        h = s.sb("h", [P, TPC, 2 * D])
        hT = s.sb("hT", [P, CE])
        ea = EdgeAttr(s, edge_attr, 18, 1)
        qk = s.sb("qk", [P, TPC, D])
        prod = s.sb("prod", [P, TPC, 4, 8])
        out = [s.sb(f"out{u}", [P, TPC, PAYW]) for u in range(2)]
        p_hT, p_qkv = s.ps("p_hT"), s.ps("p_qkv")
        stored = [s.sem(f"stored{u}") for u in range(2)]
        m = s.sems("h_ready h_turned hT_ready qkv_done qkv_out pay_ready dve_step act_step")
        with nc.Block() as block:
            @block.sync
            def _(sp):
                def store(i, u, n):
                    sp.wait_ge(m["pay_ready"], n)
                    sp.dma_start(pay[bass.ds(i * CE, CE), :].rearrange("(j p) f -> p j f", p=P), out[u][:]).then_inc(stored[u], 16)

                def body(i, t, u, n, first, last):
                    ea.load(sp, c, i, t, u, n, first, last)
                    if not (first and u == 0):
                        store(i - 1, 1 - u, n - 1)
                chunks(sp, c.TURNS, body)
                store(c.NCH - 1, 1, c.NCH)
                for u in range(2):
                    sp.wait_ge(stored[u], 16 * c.TURNS)

            @block.gpsimd
            def _(pool):
                ea.clear(pool)
                pool_program(pool, rows, None, c.TURNS)

            @block.scalar
            def _(act):
                step = Chain(act, m["act_step"])

                def body(i, t, u, n, first, last):
                    if u == 0:
                        step.restart(first)
                    ea.scalar(act, n)
                    sec.scalar(act, step, c, n)
                    norm.scalar(act, step, n, c.eps)
                    act.wait_ge(m["h_turned"], n)
                    act.activation(hT[:], p_hT[:], ACT.Copy).then_inc(m["hT_ready"], 1)
                    if not first:
                        act.wait_ge(stored[u], 16 * t)
                    act.wait_ge(m["qkv_done"], n)
                    v = p_qkv[:].rearrange("p (j f) -> p j f", j=TPC)
                    act.activation(out[u][:, :, 0:D], v[:, :, D:P], ACT.Copy)
                    act.activation(qk[:], v[:, :, 0:D], ACT.Copy).then_inc(m["qkv_out"], 1)
                chunks(act, c.TURNS, body)

            @block.vector
            def _(dve):
                step = Chain(dve, m["dve_step"])

                def body(i, t, u, n, first, last):
                    if u == 0:
                        step.restart(first)
                    dve.wait_ge(rows.gathered[u], rows.per * (t + 1))
                    buf = rows.buf[u][:].rearrange("p j (a f) -> p (j a) f", f=P)
                    sec.vector(dve, step, c, n, buf)
                    dve.sem_inc(rows.rows_free, 1)
                    norm.vector(dve, step, n, sec.x2[:], [(h[:].rearrange("p j (a f) -> p (j a) f", f=D), None)])
                    dve.sem_inc(m["h_ready"], 1)
                    if not first:
                        dve.wait_ge(stored[u], 16 * t)
                    step(dve.tensor_copy(out[u][:, :, D + 4:PAYW], sec.x2[:].rearrange("p (j a) f -> p j a f", a=2)[:, :, 0, :]))
                    dve.wait_ge(m["qkv_out"], n)
                    step(dve.tensor_tensor(prod[:].rearrange("p j h f -> p j (h f)"), qk[:, :, 0:32], qk[:, :, 32:64], ALU.mult))
                    step(dve.tensor_reduce(out[u][:, :, D:D + 4], prod[:], AX, ALU.add))
                    dve.sem_inc(m["pay_ready"], 1)
                chunks(dve, c.TURNS, body)

            @block.tensor
            def _(pe):
                def body(i, t, u, n, first, last):
                    ea.tensor(pe, c, n, t, u, first and u == 0)
                    pe.wait_ge(m["h_ready"], n)
                    for j in range(TPC):
                        ins = pe.transpose(p_hT[:, j * P:(j + 1) * P], h[:, j, :], c.ident[:])
                    ins.then_inc(m["h_turned"], 1)
                    hold(pe, m["hT_ready"], n)
                    hold(pe, ea.ready, n)
                    for j in range(TPC):
                        at = slice(j * P, (j + 1) * P)
                        pe.matmul(p_qkv[:, at], hT[:, at], c.w_qkv[:], start=True, stop=False)
                        ins = pe.matmul(p_qkv[:, at], ea.T[0:19, at], c.w_rpe[:], start=False, stop=True)
                    ins.then_inc(m["qkv_done"], 1)
                chunks(pe, c.TURNS, body)


def conv_rpe(nc, c, dram, pay, xd):
    with Scope(nc, "l2s") as s:
        rows = Rows(s, [(pay, PAYW, 0, c.perm)], PAYW)
        sct = Scatter(s, xd, D, c.scat_s, c.N)
        sm = Softmax(s)
        vT = s.sb("vT", [D + 4, CE])
        p_vT, p_score = s.ps("p_vT", (D + 4, CE)), s.ps("p_score")
        m = s.sems("turned vT_ready scored scores_out dve_step")
        with nc.Block() as block:
            @block.sync
            def _(sp):
                def body(i, t, u, n, first, last):
                    sm.load(sp, i, t, u, first, dram["far_s"], n)
                chunks(sp, c.TURNS, body)

            @block.gpsimd
            def _(pool):
                pool_program(pool, rows, sct, c.TURNS)

            @block.scalar
            def _(act):
                def body(i, t, u, n, first, last):
                    act.wait_ge(m["turned"], n)
                    act.activation(vT[:], p_vT[:], ACT.Copy).then_inc(m["vT_ready"], 1)
                    act.wait_ge(m["scored"], n)
                    act.activation(sm.score[:], p_score[:], ACT.Copy).then_inc(m["scores_out"], 1)
                    sm.scalar(act, n)
                chunks(act, c.TURNS, body)

            @block.vector
            def _(dve):
                step = Chain(dve, m["dve_step"])

                def body(i, t, u, n, first, last):
                    if u == 0:
                        step.restart(first)
                    dve.wait_ge(m["scores_out"], n)
                    sm.vector(dve, step, n, t, u, first and u == 0,
                              lambda p_: dve.tensor_tensor(p_, p_, vT[0:D, :], ALU.mult))
                    sct.free(dve, t, u, first)
                    dve.wait_ge(rows.gathered[u], rows.per * (t + 1))
                    step(dve.tensor_tensor(sct.out[u][:], sm.res[:], rows.buf[u][:, :, D + 4:PAYW], ALU.add))
                    dve.sem_inc(sct.out_ready, 1)
                    dve.sem_inc(rows.rows_free, 1)
                chunks(dve, c.TURNS, body)

            @block.tensor
            def _(pe):
                def body(i, t, u, n, first, last):
                    hold(pe, rows.gathered[u], rows.per * (t + 1))
                    if not (first and u == 0):
                        hold(pe, m["vT_ready"], n - 1)
                    for j in range(TPC):
                        ins = pe.transpose(p_vT[:, j * P:(j + 1) * P], rows.buf[u][:, j, 0:D + 4], c.ident[:])
                    ins.then_inc(m["turned"], 1)
                    hold(pe, m["vT_ready"], n)
                    pe.matmul(p_score[:], c.w_head[:], vT[:], start=True, stop=True).then_inc(m["scored"], 1)
                    sm.tensor(pe, c, n, u, first and u == 0)
                chunks(pe, c.TURNS, body)


class Gru:

    def __init__(self, s, R):
        self.e = s.sb("gru_e", [P, R, P])
        self.a = s.sb("gru_a", [P, R, D])
        self.cand = s.sb("gru_cand", [P, R, D])
        self.gates_done, self.exp1, self.arg_ready, self.exp2 = (s.sem("gru_" + n) for n in ("gates_done", "exp1", "arg_ready", "exp2"))

    def scalar(self, act, n, gates):
        act.wait_ge(self.gates_done, n)
        act.activation(self.e[:], gates[:, :, 0:P], ACT.Exp, scale=-1.0).then_inc(self.exp1, 1)
        act.wait_ge(self.arg_ready, n)
        act.activation(self.cand[:], self.a[:], ACT.Exp, scale=2.0).then_inc(self.exp2, 1)

    def vector(self, dve, step, n, gates, state, out):
        e, a, cand = self.e, self.a, self.cand
        dve.wait_ge(self.exp1, n)
        step(dve.tensor_scalar(e[:], e[:], 1.0, None, ALU.add))
        step(dve.reciprocal(e[:], e[:]))
        step(dve.tensor_tensor(a[:], e[:, :, 0:D], gates[:, :, 3 * D:4 * D], ALU.mult))
        step(dve.tensor_tensor(a[:], a[:], gates[:, :, 2 * D:3 * D], ALU.add))
        dve.sem_inc(self.arg_ready, 1)
        dve.wait_ge(self.exp2, n)
        step(dve.tensor_scalar(cand[:], cand[:], 1.0, None, ALU.add))
        step(dve.reciprocal(cand[:], cand[:]))
        step(dve.tensor_scalar(cand[:], cand[:], -2.0, 1.0, ALU.mult, ALU.add))
        if state is None:
            step(dve.tensor_tensor(a[:], e[:, :, D:P], cand[:], ALU.mult))
            step(dve.tensor_tensor(out, cand[:], a[:], ALU.subtract))
        else:
            step(dve.tensor_tensor(a[:], state, cand[:], ALU.subtract))
            step(dve.tensor_tensor(a[:], a[:], e[:, :, D:P], ALU.mult))
            step(dve.tensor_tensor(out, cand[:], a[:], ALU.add))


def quiet_states(nc, c):
    c.quiet = [c.scope.sb(f"quiet{k}", [P, D]) for k in range(2)]
    with Scope(nc, "q") as s:
        st = s.sb("st", [P, P])
        p_g, p_t = s.ps("p_g"), s.ps("p_t")
        gru = Gru(s, 1)
        dve_step, turned, q_ready, st_ready = s.sem("dve_step"), s.sem("turned"), s.sem("q_ready"), s.sem("st_ready")
        pair = s.sb("pair", [P, P])
        gates = p_g[:, 0:4 * D].rearrange("p (a f) -> p a f", a=1)
        with nc.Block() as block:
            @block.tensor
            def _(pe):
                for k in range(2):
                    if k:
                        pe.wait_ge(q_ready, 1)
                        pe.transpose(p_t[:, 0:P], pair[:], c.ident[:]).then_inc(turned, 1)
                        pe.wait_ge(st_ready, 1)
                        pe.matmul(gates[:, 0, :], st[:], c.w_gate[:], start=True, stop=False)
                    pe.matmul(gates[:, 0, :], c.ones_row[:], c.b_gate[:], start=not k, stop=True).then_inc(gru.gates_done, 1)

            @block.scalar
            def _(act):
                for k in range(2):
                    gru.scalar(act, k + 1, gates)

            @block.vector
            def _(dve):
                step = Chain(dve, dve_step)
                step(dve.memset(pair[:], 0.0))
                for k in range(2):
                    one = lambda q: q[:].rearrange("p (a f) -> p a f", a=1)
                    if k:
                        step(dve.tensor_copy(pair[:, D:P], c.quiet[0][:]))
                        dve.sem_inc(q_ready, 1)
                        dve.wait_ge(turned, 1)
                        step(dve.tensor_copy(st[:], p_t[:, 0:P]))
                        dve.sem_inc(st_ready, 1)
                    gru.vector(dve, step, k + 1, gates, one(c.quiet[0]) if k else None, one(c.quiet[k]))


def conv_rgcn(nc, c, name, dram, table, k, g_rows, out_table):
    with Scope(nc, name) as s:
        rows = Rows(s, [(table, D, 0, c.idx_src)], D)
        sct = Scatter(s, out_table, D, c.scat_d, c.N)
        norm = Norm(s, "n", TPC) if k == 0 else None
        keep = [s.sb(f"keep{u}", [D, CE]) for u in range(2)]
        hm = s.sb("hm", [P, TPC, 3 * D])
        st_rows = [s.sb(f"st_rows{u}", [P, TPC, D]) for u in range(2)]
        h01, h2 = s.sb("h01", [P, CE]), s.sb("h2", [D, CE])
        acc = [s.sb(f"acc{u}", [P, CE]) for u in range(2)]
        pair = s.sb("pair", [P, TPC, P])
        gru = Gru(s, TPC)
        stat = Stats(s) if k else None
        sums = s.sb("sums", [P, TPC, P])
        last = s.sb("last", [P, TPC])
        w = s.sb("w", [P, TPC, c.NREL])
        p_01, p_2, p_msg, p_gate = s.ps("p_01"), s.ps("p_2"), s.ps("p_msg", (D, CE)), s.ps("p_gate", (P, 2 * CE))
        gates = p_gate[:].rearrange("p (j f) -> p j f", j=TPC)
        keep_loaded = [s.sem(f"keep_loaded{u}") for u in range(2)]
        st_loaded = [s.sem(f"st_loaded{u}") for u in range(2)]
        g_stored = [s.sem(f"g_stored{u}") for u in range(2)]
        m = s.sems("hm_ready turned h_out msg_done acc_ready sums_ready sums_added dve_step act_step gates_used")
        with nc.Block() as block:
            @block.sync
            def _(sp):
                def g_store(i, u, n):
                    sp.wait_ge(sct.out_ready, n)
                    sp.dma_start(g_rows[bass.ds(i * CE, CE), :].rearrange("(j p) f -> p j f", p=P), sct.out[u][:]).then_inc(g_stored[u], 16)

                def body(i, t, u, n, first, last_):
                    if not first:
                        sp.wait_ge(sct.out_ready, n - 2)
                    sp.dma_start(keep[u][:], dram["keep_d"][bass.ds(i * CE, CE)].rearrange("(a f) -> a f", a=1).to_broadcast([D, CE])
                                 ).then_inc(keep_loaded[u], 16)
                    if k:
                        sp.dma_start(st_rows[u][:], g_rows[bass.ds(i * CE, CE), :].rearrange("(j p) f -> p j f", p=P)).then_inc(st_loaded[u], 16)
                    elif not (first and u == 0):
                        g_store(i - 1, 1 - u, n - 1)
                chunks(sp, c.TURNS, body)
                if k == 0:
                    g_store(c.NCH - 1, 1, c.NCH)
                    for u in range(2):
                        sp.wait_ge(g_stored[u], 16 * c.TURNS)

            @block.gpsimd
            def _(pool):
                pool_program(pool, rows, sct, c.TURNS)

            @block.scalar
            def _(act):
                step = Chain(act, m["act_step"])

                def body(i, t, u, n, first, last_):
                    if u == 0:
                        step.restart(first)
                    if norm:
                        norm.scalar(act, step, n, c.eps)
                    act.wait_ge(m["turned"], n)
                    act.activation(h01[:], p_01[:], ACT.Copy)
                    if k:
                        act.activation(acc[u][D:P, :], p_2[D:P, :], ACT.Copy)
                    act.activation(h2[:], p_2[0:D, :], ACT.Copy).then_inc(m["h_out"], 1)
                    gru.scalar(act, n, gates)
                chunks(act, c.TURNS, body)
                if stat:
                    stat.scalar(act, c)

            @block.vector
            def _(dve):
                step = Chain(dve, m["dve_step"])
                if k == 0:
                    step(dve.memset(pair[:], 0.0))
                    for u in range(2):
                        step(dve.memset(acc[u][D:P, :], 0.0))

                def body(i, t, u, n, first, last_):
                    if u == 0:
                        step.restart(first)
                    buf = rows.buf[u]
                    step(dve.tensor_copy(w[:], c.wrel[:, bass.ds(i * TPC, TPC), :]))
                    dve.wait_ge(rows.gathered[u], rows.per * (t + 1))
                    outs = [hm[:, :, 0:D], hm[:, :, D:P], pair[:, :, 0:D]]
                    if norm:
                        norm.vector(dve, step, n, buf[:], [(o, w[:, :, r]) for r, o in enumerate(outs)])
                    else:
                        for r, o in enumerate(outs):
                            step(dve.tensor_tensor(o, buf[:], rows4(w[:, :, r]), ALU.mult))
                        dve.wait_ge(st_loaded[u], 16 * (t + 1))
                        step(dve.tensor_copy(pair[:, :, D:P], st_rows[u][:]))
                    dve.sem_inc(m["hm_ready"], 1)
                    dve.sem_inc(rows.rows_free, 1)
                    dve.wait_ge(keep_loaded[u], 16 * (t + 1))
                    dve.wait_ge(m["msg_done"], n)
                    step(dve.tensor_tensor_scan(acc[u][0:D, :], keep[u][:], p_msg[:],
                                                0.0 if (first and u == 0) else acc[1 - u][0:D, CE - 1:CE], ALU.mult, ALU.add))
                    dve.sem_inc(m["acc_ready"], 1)
                    sct.free(dve, t, u, first)
                    if k == 0 and not first:
                        dve.wait_ge(g_stored[u], 16 * t)
                    gru.vector(dve, step, n, gates, st_rows[u][:] if k else None, sct.out[u][:])
                    if stat:
                        if not (first and u == 0):
                            dve.wait_ge(m["sums_added"], n - 1)
                        step(dve.tensor_copy(last[:], c.last_d[:, bass.ds(i * TPC, TPC)]))
                        step(dve.tensor_tensor(sums[:, :, 0:D], sct.out[u][:], over_rows(c.quiet[1][:], TPC), ALU.subtract))
                        step(dve.tensor_tensor(sums[:, :, D:P], sums[:, :, 0:D], sums[:, :, 0:D], ALU.mult))
                        dve.sem_inc(m["sums_ready"], 1)
                    dve.sem_inc(sct.out_ready, 1)
                chunks(dve, c.TURNS, body)
                if stat:
                    stat.vector(dve, Chain(dve, stat.step), c, c.gamma3, c.beta3, c.quiet[1], c.scale3, c.shift3)

            @block.tensor
            def _(pe):
                if stat:
                    stat.begin(pe, c)

                def body(i, t, u, n, first, last_):
                    hold(pe, m["hm_ready"], n)
                    for j in range(TPC):
                        at = slice(j * P, (j + 1) * P)
                        pe.transpose(p_01[:, at], hm[:, j, 0:P], c.ident[:])
                        ins = pe.transpose(p_2[:, at], pair[:, j, :], c.ident[:])
                    ins.then_inc(m["turned"], 1)
                    hold(pe, m["h_out"], n)
                    pe.matmul(p_msg[:], c.w_rel01[:], h01[:], start=True, stop=False)
                    pe.matmul(p_msg[:], c.w_rel2[:], h2[:], start=False, stop=True).then_inc(m["msg_done"], 1)
                    hold(pe, m["acc_ready"], n)
                    if not (first and u == 0):
                        hold(pe, sct.out_ready, n - 1)
                    for j in range(TPC):
                        pe.matmul(gates[:, j, :], acc[u][:, j * P:(j + 1) * P], c.w_gate[:], start=True, stop=False)
                        ins = pe.matmul(gates[:, j, :], c.ones_row[:], c.b_gate[:], start=False, stop=True)
                    ins.then_inc(gru.gates_done, 1)
                    if stat:
                        hold(pe, m["sums_ready"], n)
                        stat.add(pe, last, sums, m["sums_added"])
                chunks(pe, c.TURNS, body)
                if stat:
                    stat.finish(pe, c)


def dense_last(nc, c, xd, go, out):
    with Scope(nc, "dl") as s:
        xin = [s.sb(f"xin{u}", [P, NR, D]) for u in range(2)]
        gin = [s.sb(f"gin{u}", [P, NR, D]) for u in range(2)]
        res = [s.sb(f"res{u}", [P, NR, D]) for u in range(2)]
        loaded = [s.sem(f"loaded{u}") for u in range(2)]
        stored = [s.sem(f"stored{u}") for u in range(2)]
        done, dve_step = s.sem("done"), s.sem("dve_step")
        with nc.Block() as block:
            @block.sync
            def _(sp):
                def store(i, u, n, parts):
                    sp.wait_ge(done, n)
                    sp.dma_start(node_rows(out, i, parts, D), res[u][0:parts]).then_inc(stored[u], 16)

                def body(i, t, u, n, first, parts):
                    if not first:
                        sp.wait_ge(done, n - 2)
                    sp.dma_start(xin[u][0:parts], node_rows(xd, i, parts, D)).then_inc(loaded[u], 16)
                    sp.dma_start(gin[u][0:parts], node_rows(go, i, parts, D)).then_inc(loaded[u], 16)
                    if not (first and u == 0):
                        store(i - 1, 1 - u, n - 1, P)
                node_chunks(sp, c, body)
                store(c.NCH - 1, 1, c.NCH, (c.N - (c.NCH - 1) * P * NR) // NR)
                for u in range(2):
                    sp.wait_ge(stored[u], 16 * c.TURNS)

            @block.vector
            def _(dve):
                step = Chain(dve, dve_step)

                def body(i, t, u, n, first, p):
                    if u == 0:
                        step.restart(first)
                    dve.wait_ge(loaded[u], 32 * (t + 1))
                    if not first:
                        dve.wait_ge(stored[u], 16 * t)
                    r = res[u][0:p]
                    step(dve.tensor_tensor(r, gin[u][0:p], over_rows(c.scale3[0:p, :], NR), ALU.mult))
                    step(dve.tensor_tensor(xin[u][0:p], xin[u][0:p], over_rows(c.shift3[0:p, :], NR), ALU.add))
                    step(dve.tensor_tensor(r, r, xin[u][0:p], ALU.add))
                    dve.sem_inc(done, 1)
                node_chunks(dve, c, body)


class Common:
    pass


def gnn(nc, a, out):
    c = Common()
    E, N = a["src"].shape[0], a["x"].shape[0]
    c.E, c.N, c.NREL = E, N, a["L3_gnn_weight"].shape[0]
    c.NCH = -(-E // CE)
    c.NT = c.NCH * TPC
    c.TURNS = c.NCH // 2
    assert c.NCH % 2 == 0 and c.NT * P <= LIST and N < PAD_NODE and N <= SKIP

    def dram_tensor(name, shape, dt=F32):
        return nc.dram_tensor(name, shape, dt, kind="Internal").ap()

    dram = {"keys": dram_tensor("keys", (LIST + 2,)),
            "far_d": dram_tensor("far_d", (LIST,)), "keep_d": dram_tensor("keep_d", (LIST,)),
            "far_s": dram_tensor("far_s", (LIST,))}
    with Scope(nc, "all") as sc:
        c.scope = sc
        Scope.whole = sc
        c.ident = sc.sb("ident", [P, P])
        c.minus1 = sc.sb("minus1", [1, 1])
        c.idx_src, c.idx_dst, c.scat_d, c.scat_s, c.perm = (
            sc.sb(name, [P, c.NT], I32) for name in ("idx_src", "idx_dst", "scat_d", "scat_s", "perm"))
        c.last_d = sc.sb("last_d", [P, c.NT])
        c.wrel = sc.sb("wrel", [P, c.NT, c.NREL])
        c.eps = sc.sb("eps", [P, 1])
        setup(nc, c, a)
        prep_lists(nc, c, a["src"], a["dst"], a["edge_weight"], a["edge_type_3"], dram)
        x1 = dram_tensor("x1", (N, D))
        x1o = dram_tensor("x1o", (N, 2 * D))
        dense_start(nc, c, a["x"], x1, x1o)
        conv_gat(nc, c, a["x"], dram, x1)
        conv_gatv2(nc, c, dram, x1, x1o, a["edge_attr_16"])
        xd = dram_tensor("xd", (N, D))
        pay = dram_tensor("pay", (c.NCH * CE, PAYW))
        edge_qkv(nc, c, x1o, pay, a["edge_attr_18"])
        dense_second(nc, c, x1o, xd)
        conv_rpe(nc, c, dram, pay, xd)
        quiet_states(nc, c)
        g1 = dram_tensor("g1", (N, D))
        g2 = dram_tensor("g2", (N, D))
        g_rows = dram_tensor("g_rows", (c.NCH * CE, D))
        fill_rows(nc, c, "f1", g1, c.quiet[0][:])
        fill_rows(nc, c, "f2", g2, c.quiet[1][:])
        conv_rgcn(nc, c, "l3a", dram, xd, 0, g_rows, g1)
        conv_rgcn(nc, c, "l3b", dram, g1, 1, g_rows, g2)
        dense_last(nc, c, xd, g2, out)


def kernel(**inputs):
    import numpy as np
    import concourse.bacc as bacc
    from concourse.bass_utils import run_bass_kernel_spmd as run

    nc = bacc.Bacc("TRN2", target_bir_lowering=False, num_devices=1)
    arrays = {f"in_{k}": np.ascontiguousarray(v) for k, v in inputs.items()}
    ins = {k: nc.dram_tensor(f"in_{k}", arrays[f"in_{k}"].shape, mybir.dt.from_np(arrays[f"in_{k}"].dtype),
                             kind="ExternalInput").ap() for k in inputs}
    out = nc.dram_tensor("out_0", inputs["x"].shape, F32, kind="ExternalOutput").ap()
    gnn(nc, ins, out)
    return run(nc, [arrays], core_ids=[0]).results[0]["out_0"]
```

```python
from contextlib import ExitStack

import concourse.bass as bass
from concourse import mybir

F32 = mybir.dt.float32
I32 = mybir.dt.int32
ALU = mybir.AluOpType
ACT = mybir.ActivationFunctionType
AX = mybir.AxisListType.X

P = 128
D = 64
TPC = 4
CE = TPC * P
NBLK = 4
LIST = NBLK * P * P
PAD_NODE = 131071
SKIP = 1 << 20
FAR = -1.0e30
BIG = 2.0 ** 60
LN_EPS = 1e-5
HEADS = 4
LN_EXP_SET = 6
NR = 8


class Scope:

    def __init__(self, nc, name):
        self.nc, self.name, self.stack, self.used = nc, name, ExitStack(), []

    whole = None

    def __enter__(self):
        self.stack.__enter__()
        return self

    def __exit__(self, *a):
        if self.used and a[0] is None:
            with self.nc.Block() as block:
                @block.gpsimd
                def _(pool):
                    for s in self.used:
                        pool.sem_clear(s)
        return self.stack.__exit__(*a)

    def sb(self, name, shape, dt=F32):
        return self.stack.enter_context(self.nc.sbuf_tensor(f"{self.name}_{name}", shape, dt))

    def ps(self, name, shape=(P, CE)):
        return self.stack.enter_context(self.nc.psum_tensor(f"{self.name}_{name}", list(shape), F32))

    def sem(self, name):
        s = self.stack.enter_context(self.nc.semaphore(f"{self.name}_{name}"))
        self.used.append(s)
        return s

    def swdge_sem(self, name):
        return Scope.whole.stack.enter_context(self.nc.semaphore(f"{self.name}_{name}"))

    def sems(self, names):
        return {n: self.sem(n) for n in names.split()}


class Chain:

    def __init__(self, eng, sem):
        self.eng, self.sem, self.n = eng, sem, 0

    def restart(self, first):
        if self.n or not first:
            self.eng.sem_clear(self.sem)
        self.n = 0

    def __call__(self, ins):
        self.n += 1
        ins.then_inc(self.sem, 1)
        self.eng.wait_ge(self.sem, self.n)
        return ins



class Chunk:

    def __init__(self, t, u, total):
        self.t, self.u, self.i, self.n = t, u, 2 * t + u, 2 * t + u + 1
        whole = isinstance(t, int)
        self.first = whole and t == 0
        self.start = self.first and u == 0
        self.last = whole and 2 * t + u == total - 1


def slots(eng, total, lags, body, step=None):
    turns = total // 2
    head = 1 + -(-lags // 2)

    def turn(t):
        if step:
            step.restart(isinstance(t, int) and t == 0)
        for u in range(2):
            ks = []
            for lag in range(lags + 1):
                uu, tt = (u - lag) % 2, t + (u - lag) // 2
                inside = not isinstance(t, int) or 0 <= tt < turns
                ks.append(Chunk(tt, uu, total) if inside else None)
            body(*ks)

    for t in range(head):
        turn(t)
    with eng.Fori(head, turns - 1) as t:
        turn(t)
    for t in range(turns - 1, turns + -(-lags // 2)):
        turn(t)


def hold(eng, sem, n):
    eng.wait_ge(sem, n)
    eng.nop(nofuse=True)


def load_ln_exp(nc, act):
    act.add_instruction(mybir.InstLoadActFuncSet(name=nc.get_next_instruction_name(), ins=[], outs=[], act_func_set_id=LN_EXP_SET))


def prep_lists(nc, c, src, dst, weight, etype, dram, beside):
    E = src.shape[0]
    N = c.N
    beside_act, beside_sync, beside_pool = beside
    full, rest = E // P, E % P
    blocks = [min(P, full - b * P) for b in range(NBLK)]
    with Scope(nc, "prep") as s:
        ident = c.ident
        key = [s.sb(f"key{i}", [P, NBLK * P]) for i in range(2)]
        pay = [s.sb(f"pay{i}", [P, NBLK * P]) for i in range(2)]
        swap = s.sb("swap", [P, NBLK * P // 2], I32)
        icur = s.sb("icur", [P, NBLK, P], I32)
        iprev = s.sb("iprev", [P, NBLK, P], I32)
        inext = s.sb("inext", [P, NBLK, P], I32)
        isrc = s.sb("isrc", [P, NBLK, P], I32)
        ityp = s.sb("ityp", [P, NBLK, P], I32)
        nrm = s.sb("nrm", [P, NBLK, P])
        idx_i = s.sb("idx_i", [P, NBLK * P], I32)
        cur = s.sb("cur", [P, NBLK, P])
        oth = s.sb("oth", [P, NBLK, P])
        start = s.sb("start", [P, NBLK, P])
        flag = s.sb("flag", [P, NBLK, P])
        sgn = s.sb("sgn", [P, 1])
        sgn_i = s.sb("sgn_i", [P, 1], I32)
        ptk, ptp = s.ps("ptk"), s.ps("ptp")
        filled, loaded, keys_ready, pay_copied = (s.sem(n) for n in ("filled", "loaded", "keys_ready", "pay_copied"))
        dve_step, turned, stored, last_pay, to_store = (s.sem(n) for n in ("dve_step", "turned", "stored", "last_pay", "to_store"))
        keys_stored, keys_back, pool_step = s.sem("keys_stored"), s.sem("keys_back"), s.sem("pool_step")

        levels = [(k, j) for k in range(1, 17) for j in range(k - 1, -1, -1)]
        n_stage = len(levels)
        with nc.Block() as block:

            @block.gpsimd
            def _(pool):
                pool.memset(icur[:], PAD_NODE).then_inc(filled, 1)
                pool.memset(iprev[:], PAD_NODE).then_inc(filled, 1)
                pool.memset(inext[:], PAD_NODE).then_inc(filled, 1)
                pool.memset(isrc[:], PAD_NODE).then_inc(filled, 1)
                pool.memset(ityp[:], 0).then_inc(filled, 1)
                pool.memset(nrm[:], 0.0).then_inc(filled, 1)
                pool.iota(idx_i[:].rearrange("p (b f) -> p b f", b=NBLK), pattern=[[P * P, NBLK], [1, P]],
                          base=0, channel_multiplier=P).then_inc(filled, 1)
                pool.iota(sgn_i[:], pattern=[[0, 1]], base=0, channel_multiplier=1).then_inc(filled, 1)
                pool.wait_ge(filled, 8)
                pool.memset(iprev[0:1, 0, 0:1], -1).then_inc(filled, 1)
                beside_pool(pool)

            loads = []

            @block.sync
            def _(sp):
                sp.wait_ge(filled, 9)
                n = 0
                for tile_, vec in ((isrc, src), (icur, dst), (ityp, etype), (nrm, weight)):
                    for b, rows in enumerate(blocks):
                        sp.dma_start(tile_[0:rows, b, :], vec[b * P * P:b * P * P + rows * P].rearrange("(r f) -> r f", f=P)).then_inc(loaded, 16)
                        n += 1
                    sp.dma_start(tile_[blocks[-1]:blocks[-1] + 1, NBLK - 1, 0:rest], vec[full * P:E].rearrange("(r f) -> r f", r=1)).then_inc(loaded, 16)
                    n += 1
                for b, rows in enumerate(blocks):
                    sp.dma_start(inext[0:rows, b, :], dst[b * P * P + 1:b * P * P + rows * P + 1].rearrange("(r f) -> r f", f=P)).then_inc(loaded, 16)
                    lo = 1 if b == 0 else 0
                    sp.dma_start(iprev[lo:rows, b, :], dst[(b * P + lo) * P - 1:(b * P + rows) * P - 1].rearrange("(r f) -> r f", f=P)).then_inc(loaded, 16)
                    n += 2
                sp.dma_start(iprev[0:1, 0, 1:P], dst[0:P - 1].rearrange("(r f) -> r f", r=1)).then_inc(loaded, 16)
                sp.dma_start(inext[blocks[-1]:blocks[-1] + 1, NBLK - 1, 0:rest - 1], dst[full * P + 1:E].rearrange("(r f) -> r f", r=1)).then_inc(loaded, 16)
                sp.dma_start(iprev[blocks[-1]:blocks[-1] + 1, NBLK - 1, 0:rest], dst[full * P - 1:E - 1].rearrange("(r f) -> r f", r=1)).then_inc(loaded, 16)
                loads.append(n + 3)
                beside_sync(sp)
                sp.wait_ge(to_store, 1)
                sp.dma_start(dram["far_d"].rearrange("(b p f) -> p b f", p=P, f=P), start[:]).then_inc(stored, 16)
                sp.dma_start(dram["keep_d"].rearrange("(b p f) -> p b f", p=P, f=P), flag[:]).then_inc(stored, 16)
                sp.wait_ge(to_store, 2)
                sp.dma_start(dram["keys"][1:LIST + 1].rearrange("(b p f) -> p b f", p=P, f=P), cur[:]).then_inc(keys_stored, 16)
                sp.dma_start(dram["keys"][0:1].rearrange("(r f) -> r f", r=1), c.minus1[0:1, 0:1]).then_inc(keys_stored, 16)
                sp.dma_start(dram["keys"][LIST + 1:LIST + 2].rearrange("(r f) -> r f", r=1), c.minus1[0:1, 0:1]).then_inc(keys_stored, 16)
                sp.wait_ge(keys_stored, 48)
                sp.dma_start(oth[:], dram["keys"][0:LIST].rearrange("(b p f) -> p b f", p=P, f=P)).then_inc(keys_back, 16)
                sp.dma_start(nrm[:], dram["keys"][2:LIST + 2].rearrange("(b p f) -> p b f", p=P, f=P)).then_inc(keys_back, 16)
                sp.wait_ge(to_store, 3)
                sp.dma_start(dram["far_s"].rearrange("(b p f) -> p b f", p=P, f=P), start[:]).then_inc(stored, 16)
                sp.wait_ge(stored, 48)

            @block.scalar
            def _(act):
                beside_act(act)
                for n in range(n_stage):
                    act.wait_ge(keys_ready, n + 1)
                    act.activation(pay[(n + 1) % 2][:], pay[n % 2][:], ACT.Copy).then_inc(pay_copied, 1)

            @block.vector
            def _(dve):
                step = Chain(dve, dve_step)
                flips = [0]

                def turned_rows(view_in, out):
                    flips[0] += 1
                    dve.wait_ge(turned, flips[0])
                    step(dve.tensor_copy(out, ptk[:]))

                dve.wait_ge(loaded, 16 * loads[0])
                dve.wait_ge(filled, 9)
                flat = lambda a: a[:].rearrange("p b f -> p (b f)")
                step(dve.tensor_copy(flat(cur), flat(icur)))
                step(dve.tensor_copy(flat(oth), flat(iprev)))
                step(dve.tensor_tensor(flat(start), flat(cur), flat(oth), ALU.not_equal))
                step(dve.tensor_scalar(flat(flag), flat(start), -1.0, 1.0, ALU.mult, ALU.add))
                step(dve.tensor_scalar(flat(start), flat(start), FAR, None, ALU.mult))
                dve.sem_inc(to_store, 1)
                step(dve.tensor_copy(flat(oth), flat(inext)))
                step(dve.tensor_tensor(key[1][:], flat(cur), flat(oth), ALU.not_equal))

                def to_columns(rows, out):
                    flips[0] += 1
                    step(dve.tensor_copy(pay[1][:], rows))
                    dve.sem_inc(last_pay, 1)
                    dve.wait_ge(turned, flips[0])
                    step(dve.tensor_copy(out, ptk[:, 0:c.NT] if out.shape[-1] == c.NT else ptk[:]))

                to_columns(key[1][:], c.last_d[:])
                step(dve.tensor_scalar(key[0][:], key[1][:], -float(SKIP), float(SKIP), ALU.mult, ALU.add))
                step(dve.tensor_tensor(key[0][:], key[0][:], flat(cur), ALU.add))
                to_columns(key[0][:], c.scat_d[:])
                for lst, out in ((icur, c.idx_dst), (isrc, c.idx_src)):
                    step(dve.tensor_copy(key[0][:], flat(lst)))
                    step(dve.tensor_scalar(key[1][:], key[0][:], float(N) - 0.5, None, ALU.is_lt))
                    step(dve.tensor_tensor(key[0][:], key[0][:], key[1][:], ALU.mult))
                    to_columns(key[0][:], out[:])
                for r in range(c.NREL):
                    step(dve.tensor_copy(key[0][:], flat(ityp)))
                    step(dve.tensor_scalar(key[0][:], key[0][:], float(r), None, ALU.is_equal))
                    step(dve.tensor_tensor(key[0][:], key[0][:], flat(nrm), ALU.mult))
                    to_columns(key[0][:], c.wrel[:, :, r])

                step(dve.tensor_copy(key[0][:], flat(isrc)))
                step(dve.tensor_copy(pay[0][:], idx_i[:]))
                step(dve.tensor_scalar(sgn_i[:], sgn_i[:], 1, None, ALU.bitwise_and))
                step(dve.tensor_scalar(sgn[:], sgn_i[:], -2.0, 1.0, ALU.mult, ALU.add))

                def descending(k, at, layout):
                    if k == 16:
                        return
                    if k == 7:
                        step(dve.tensor_scalar(at[:], at[:], sgn[:, 0:1], None, ALU.mult))
                        return
                    d = 1 << (k if layout == "T" else k - 7)
                    v = at[:].rearrange("p (n two d) -> p n two d", two=2, d=d)[:, :, 1, :]
                    step(dve.tensor_scalar(v, v, -1.0, None, ALU.mult))

                layout = "T"
                for n, (k, j) in enumerate(levels):
                    kin, kout, pin, pout = key[n % 2], key[(n + 1) % 2], pay[n % 2], pay[(n + 1) % 2]
                    need = "T" if j < 7 else "A"
                    if need != layout:
                        dve.sem_inc(last_pay, 1)
                        flips[0] += 1
                        dve.wait_ge(turned, flips[0])
                        step(dve.tensor_copy(kin[:], ptk[:]))
                        step(dve.tensor_copy(pin[:], ptp[:]))
                        layout = need
                    if j == k - 1:
                        if k > 8:
                            descending(k - 1, kin, layout)
                        descending(k, kin, layout)
                    d = 1 << (j if layout == "T" else j - 7)
                    pair = lambda a: a[:].rearrange("p (n two d) -> p n two d", two=2, d=d)
                    a, b = pair(kin)[:, :, 0, :], pair(kin)[:, :, 1, :]
                    m = swap[:].rearrange("p (n d) -> p n d", d=d)
                    dve.sem_inc(keys_ready, 1)
                    step(dve.tensor_tensor(m, a, b, ALU.is_gt))
                    dve.tensor_tensor(pair(kout)[:, :, 0, :], a, b, ALU.min)
                    step(dve.tensor_tensor(pair(kout)[:, :, 1, :], a, b, ALU.max))
                    dve.wait_ge(pay_copied, n + 1)
                    dve.copy_predicated(pair(pout)[:, :, 0, :], m, pair(pin)[:, :, 1, :])
                    step(dve.copy_predicated(pair(pout)[:, :, 1, :], m, pair(pin)[:, :, 0, :]))
                    if j == 0 and k < 8:
                        descending(k, kout, layout)

                dve.wait_ge(stored, 32)
                step(dve.tensor_copy(flat(cur), key[n_stage % 2][:]))
                dve.sem_inc(to_store, 1)
                dve.wait_ge(keys_back, 32)
                step(dve.tensor_tensor(flat(start), flat(cur), flat(oth), ALU.not_equal))
                step(dve.tensor_scalar(flat(start), flat(start), FAR, None, ALU.mult))
                dve.sem_inc(to_store, 1)
                spare = key[(n_stage + 1) % 2]
                step(dve.tensor_tensor(spare[:], flat(cur), flat(nrm), ALU.not_equal))
                step(dve.tensor_scalar(spare[:], spare[:], -float(SKIP), float(SKIP), ALU.mult, ALU.add))
                step(dve.tensor_tensor(spare[:], spare[:], flat(cur), ALU.add))
                step(dve.tensor_scalar(flat(oth), pay[n_stage % 2][:], E - 0.5, None, ALU.is_lt))
                step(dve.tensor_tensor(flat(oth), pay[n_stage % 2][:], flat(oth), ALU.mult))
                to_columns(spare[:], c.scat_s[:])
                to_columns(oth[:].rearrange("p b f -> p (b f)"), c.perm[:])

            @block.tensor
            def _(pe):
                n = 0

                def flip(psum, rows):
                    for b in range(NBLK):
                        ins = pe.transpose(psum[:, b * P:(b + 1) * P], rows[:, b * P:(b + 1) * P], ident[:])
                    return ins

                for _ in range(4 + c.NREL):
                    n += 1
                    pe.wait_ge(last_pay, n)
                    flip(ptk, pay[1]).then_inc(turned, 1)
                layout = "T"
                for m, (k, j) in enumerate(levels):
                    need = "T" if j < 7 else "A"
                    if need != layout:
                        n += 1
                        pe.wait_ge(last_pay, n)
                        flip(ptk, key[m % 2])
                        flip(ptp, pay[m % 2]).then_inc(turned, 1)
                        layout = need
                for _ in range(2):
                    n += 1
                    pe.wait_ge(last_pay, n)
                    flip(ptk, pay[1]).then_inc(turned, 1)


def setup(nc, c, w):
    sc = c.scope
    c.w_val0 = sc.sb("w_val0", [D, D])
    c.w_att0 = sc.sb("w_att0", [P, P])
    c.bias0 = sc.sb("bias0", [P, D])
    c.w_lr = sc.sb("w_lr", [P, 2, D])
    c.w_e1 = sc.sb("w_e1", [16, 2, D])
    c.b_g1 = sc.sb("b_g1", [P, 1])
    c.b_l1 = sc.sb("b_l1", [D, 1])
    c.w_att1 = sc.sb("w_att1", [P, P])
    c.bias1 = sc.sb("bias1", [P, D])
    c.gamma1, c.beta1 = sc.sb("gamma1", [P, D]), sc.sb("beta1", [P, D])
    c.w_qkv = sc.sb("w_qkv", [P, P])
    c.w_rpe = sc.sb("w_rpe", [19, P])
    c.w_head = sc.sb("w_head", [D + 4, P])
    c.w_rel01, c.w_rel2 = sc.sb("w_rel01", [P, D]), sc.sb("w_rel2", [D, D])
    c.w_gate = sc.sb("w_gate", [P, 4 * D])
    c.b_gate = sc.sb("b_gate", [1, 4 * D])
    c.gamma3, c.beta3 = sc.sb("gamma3", [P, D]), sc.sb("beta3", [P, D])
    c.scale1, c.shift1, c.scale3, c.shift3 = (sc.sb(n, [P, D]) for n in ("scale1", "shift1", "scale3", "shift3"))
    c.zero_col = sc.sb("zero_col", [P, 1])
    c.ones_row = sc.sb("ones_row", [1, P])
    scale = float(8) ** -0.5
    with Scope(nc, "setup") as s:
        wt = s.sb("wt", [D, 2, D])
        att_s, att_d = s.sb("att_s", [D, 1]), s.sb("att_d", [D, 1])
        head8 = s.sb("head8", [P, P])
        att_w = s.sb("att_w", [D, 2, P])
        att1, b_l, b_r = (s.sb(n, [P, 1]) for n in ("att1", "b_l", "b_r"))
        brow = s.sb("brow", [1, 2, P])
        grow = s.sb("grow", [1, 2, 3 * D])
        gates = s.sb("gates", [D, 3, P])
        pa, pb, pc, pg = s.ps("pa"), s.ps("pb"), s.ps("pc"), s.ps("pg")
        filled, loaded, step_s, trans, prods, ready = (s.sem(n) for n in ("filled", "loaded", "step", "trans", "prods", "ready"))
        loads = []
        with nc.Block() as block:
            @block.gpsimd
            def _(pool):
                pool.memset(c.ident[:], 0.0).then_inc(filled, 1)
                pool.memset(c.w_qkv[:], 0.0).then_inc(filled, 1)
                pool.memset(c.w_gate[:], 0.0).then_inc(filled, 1)
                pool.memset(c.w_head[:], 1.0).then_inc(filled, 1)
                pool.memset(head8[:], 1.0).then_inc(filled, 1)
                pool.memset(c.ones_row[:], 1.0).then_inc(filled, 1)
                pool.memset(c.minus1[:], -1.0).then_inc(filled, 1)
                pool.memset(c.eps[:], LN_EPS).then_inc(filled, 1)
                pool.memset(c.zero_col[:], 0.0).then_inc(filled, 1)
                pool.memset(c.one[:], 1.0).then_inc(filled, 1)
                pool.wait_ge(filled, 10)
                pool.affine_select(out=c.ident[:], in_=c.ident[:], compare_op=ALU.not_equal, fill=1.0, base=0,
                                   pattern=[[-1, P]], channel_multiplier=1).then_inc(filled, 1)
                v = c.w_head[:].rearrange("p (a h f) -> p a h f", a=2, h=4)
                pool.affine_select(out=v, in_=v, compare_op=ALU.is_equal, fill=0.0, base=-D,
                                   pattern=[[0, 2], [-1, 4], [0, 16]], channel_multiplier=1).then_inc(filled, 1)
                v = head8[:].rearrange("p (h f) -> p h f", h=8)
                pool.affine_select(out=v, in_=v, compare_op=ALU.is_ge, fill=0.0, base=0,
                                   pattern=[[-16, 8], [0, 16]], channel_multiplier=1).then_inc(filled, 1)
                pool.wait_ge(filled, 13)
                pool.affine_select(out=v, in_=v, compare_op=ALU.is_ge, fill=0.0, base=15,
                                   pattern=[[16, 8], [0, 16]], channel_multiplier=-1).then_inc(filled, 1)

            @block.sync
            def _(sp):
                sp.wait_ge(filled, 10)
                n = [0]

                def ld(out, in_):
                    sp.dma_start(out, in_).then_inc(loaded, 16)
                    n[0] += 1

                col = lambda v: v.rearrange("(p a) -> p a", a=1)
                row = lambda v: v.rearrange("(a p) -> a p", a=1)
                wide = lambda v: row(v).to_broadcast([P, D])
                ld(c.w_val0[:], w["L0_gnn_W"])
                ld(att_s[:], col(w["L0_gnn_att_src"]))
                ld(att_d[:], col(w["L0_gnn_att_dst"]))
                ld(c.bias0[:], wide(w["L0_gnn_bias"]))
                ld(c.b_l1[:], col(w["L1_gnn_b_l"]))
                for k in range(2):
                    ld(c.w_lr[0:D, k, :], w["L1_gnn_W_l"])
                    ld(c.w_lr[D:P, k, :], w["L1_gnn_W_r"])
                    ld(c.w_e1[:, k, :], w["L1_gnn_W_e"])
                    ld(b_l[k * D:(k + 1) * D, :], col(w["L1_gnn_b_l"]))
                    ld(b_r[k * D:(k + 1) * D, :], col(w["L1_gnn_b_r"]))
                    ld(att1[k * D:(k + 1) * D, :], w["L1_gnn_att"].rearrange("h (c a) -> (h c) a", a=1))
                ld(c.bias1[:], wide(w["L1_gnn_bias"]))
                ld(c.gamma1[:], wide(w["L1_gnn_gamma"]))
                ld(c.beta1[:], wide(w["L1_gnn_beta"]))
                ld(c.w_qkv[0:D, 0:32], w["L2_gnn_qkv_w"][:, 0:32])
                ld(c.w_qkv[D:P, 32:P], w["L2_gnn_qkv_w"][:, 32:P])
                ld(c.w_rpe[1:19, 0:32], w["L2_gnn_q_rpe_w"])
                ld(c.w_rpe[1:19, 32:64], w["L2_gnn_k_rpe_w"])
                ld(c.w_rpe[1:19, 64:128], w["L2_gnn_v_rpe_w"])
                ld(brow[:, 0, :], row(w["L2_gnn_qkv_b"]))
                ld(brow[:, 1, 0:32], row(w["L2_gnn_q_rpe_b"]))
                ld(brow[:, 1, 32:64], row(w["L2_gnn_k_rpe_b"]))
                ld(brow[:, 1, 64:128], row(w["L2_gnn_v_rpe_b"]))
                ld(c.w_rel01[0:D, :], w["L3_gnn_weight"][0])
                ld(c.w_rel01[D:P, :], w["L3_gnn_weight"][1])
                ld(c.w_rel2[:], w["L3_gnn_weight"][2])
                ld(gates[:, :, 0:D], w["L3_gnn_w_ih"].rearrange("(g p) f -> p g f", g=3))
                ld(gates[:, :, D:P], w["L3_gnn_w_hh"].rearrange("(g p) f -> p g f", g=3))
                ld(grow[:, 0, :], row(w["L3_gnn_b_ih"]))
                ld(grow[:, 1, :], row(w["L3_gnn_b_hh"]))
                ld(c.gamma3[:], wide(w["L3_gnn_gamma"]))
                ld(c.beta3[:], wide(w["L3_gnn_beta"]))
                loads.append(n[0])

            @block.vector
            def _(dve):
                step = Chain(dve, step_s)
                dve.wait_ge(filled, 14)
                dve.wait_ge(loaded, 16 * loads[0])
                step(dve.tensor_copy(att_w[:, 0, :], att_s[:, 0:1].to_broadcast([D, P])))
                step(dve.tensor_copy(att_w[:, 1, :], att_d[:, 0:1].to_broadcast([D, P])))
                step(dve.tensor_tensor(c.b_g1[:], b_l[:], b_r[:], ALU.add))
                for a in range(2):
                    step(dve.tensor_tensor(c.w_att1[:, a * D:(a + 1) * D], head8[:, 0:D], head8[:, D:P], ALU.add))
                step(dve.tensor_scalar(c.w_att1[:], c.w_att1[:], att1[:, 0:1], None, ALU.mult))
                step(dve.tensor_scalar(c.w_att1[0:D, :], c.w_att1[0:D, :], 0.2, None, ALU.mult))
                step(dve.tensor_scalar(c.w_att1[D:P, :], c.w_att1[D:P, :], 0.8, None, ALU.mult))
                step(dve.tensor_scalar(c.w_qkv[0:D, 0:32], c.w_qkv[0:D, 0:32], scale, None, ALU.mult))
                step(dve.tensor_scalar(brow[:, 0, 0:32], brow[:, 0, 0:32], scale, None, ALU.mult))
                step(dve.tensor_tensor(c.w_rpe[0:1, :], brow[:, 0, :], brow[:, 1, :], ALU.add))
                step(dve.tensor_tensor(c.b_gate[:, 0:2 * D], grow[:, 0, 0:2 * D], grow[:, 1, 0:2 * D], ALU.add))
                step(dve.tensor_copy(c.b_gate[:, 2 * D:3 * D], grow[:, 0, 2 * D:3 * D]))
                step(dve.tensor_copy(c.b_gate[:, 3 * D:4 * D], grow[:, 1, 2 * D:3 * D]))
                dve.wait_ge(trans, 1)
                step(dve.tensor_copy(wt[:, 0, :], pa[0:D, 0:D]))
                step(dve.tensor_copy(wt[:, 1, :], pa[0:D, 0:D]))
                step(dve.tensor_copy(c.w_gate[:, 0:2 * D], pg[:, 0:2 * D]))
                step(dve.tensor_copy(c.w_gate[0:D, 2 * D:3 * D], pg[0:D, 2 * D:3 * D]))
                step(dve.tensor_copy(c.w_gate[D:P, 3 * D:4 * D], pg[D:P, 2 * D:3 * D]))
                dve.sem_inc(ready, 1)
                dve.wait_ge(prods, 1)
                step(dve.tensor_copy(c.w_att0[0:D, :], pb[0:D, 0:P]))
                step(dve.tensor_copy(c.w_att0[D:P, :], pc[D:P, 0:P]))

            @block.tensor
            def _(pe):
                pe.wait_ge(filled, 14)
                pe.wait_ge(loaded, 16 * loads[0])
                pe.transpose(pa[0:D, 0:D], c.w_val0[:], c.ident[0:D, 0:D])
                for g in range(3):
                    ins = pe.transpose(pg[:, g * D:(g + 1) * D], gates[:, g, :], c.ident[0:D, 0:D])
                ins.then_inc(trans, 1)
                pe.wait_ge(ready, 1)
                both = wt[:].rearrange("p a f -> p (a f)")
                pe.matmul(pb[:, 0:P], both, att_w[:, 0, :], start=True, stop=True)
                pe.matmul(pc[:, 0:P], both, att_w[:, 1, :], start=True, stop=True).then_inc(prods, 1)


def rows4(v):
    return v.unsqueeze(2).to_broadcast([v.shape[0], v.shape[1], D])


def over_rows(v, n):
    return v.unsqueeze(1).to_broadcast([v.shape[0], n, v.shape[1]])




class Norm:

    def __init__(self, s, name, R):
        self.mean, self.var, self.lnv, self.rstd = (s.sb(f"{name}_{n}", [P, R]) for n in ("mean", "var", "lnv", "rstd"))
        self.cen = s.sb(f"{name}_cen", [P, R, D])
        self.sq = s.sb(f"{name}_sq", [P, R, D])
        self.centered, self.squared, self.summed, self.scaled = (s.sem(f"{name}_{n}") for n in ("centered", "squared", "summed", "scaled"))

    def center(self, dve, step, x, p=P):
        step(dve.tensor_reduce(self.mean[0:p, :], x, AX, ALU.add))
        step(dve.scalar_tensor_tensor(self.cen[0:p], rows4(self.mean[0:p, :]), -1.0 / D, x, ALU.mult, ALU.add))
        dve.sem_inc(self.centered, 1)

    def square(self, act, n, p=P):
        act.wait_ge(self.centered, n)
        act.activation(self.sq[0:p], self.cen[0:p], ACT.Square).then_inc(self.squared, 1)

    def add_up(self, dve, step, n, p=P):
        dve.wait_ge(self.squared, n)
        step(dve.tensor_reduce(self.var[0:p, :], self.sq[0:p], AX, ALU.add))
        dve.sem_inc(self.summed, 1)

    def rsqrt(self, act, step, c, n, p=P):
        act.wait_ge(self.summed, n)
        step(act.activation(self.lnv[0:p, :], self.var[0:p, :], ACT.Ln, bias=c.eps[0:p, 0:1], scale=1.0 / D))
        act.activation(self.rstd[0:p, :], self.lnv[0:p, :], ACT.Exp, scale=-0.5).then_inc(self.scaled, 1)

    def scale(self, dve, step, n, out, p=P):
        dve.wait_ge(self.scaled, n)
        step(dve.scalar_tensor_tensor(out, self.cen[0:p], 0.0, rows4(self.rstd[0:p, :]), ALU.max, ALU.mult))


class Softmax:

    def __init__(self, s):
        self.far = [s.sb(f"far{u}", [P, CE]) for u in range(2)]
        self.top = [s.sb(f"top{u}", [P, CE + 1]) for u in range(2)]
        self.ex = s.sb("ex", [P, 2, CE])
        self.sums = [s.sb(f"sums{u}", [P, CE]) for u in range(2)]
        self.rden = s.sb("rden", [P, TPC, HEADS])
        self.p_sums = s.ps("p_sums")
        self.far_loaded = [s.sem(f"far_loaded{u}") for u in range(2)]
        self.far_used, self.shifted, self.exped, self.summed, self.sums_turned = (
            s.sem(n) for n in ("far_used", "shifted", "exped", "run_summed", "sums_turned"))

    def load(self, sp, k, row):
        if not k.first:
            sp.wait_ge(self.far_used, k.n - 2)
        sp.dma_start(self.far[k.u][:], row[bass.ds(k.i * CE, CE)].rearrange("(a f) -> a f", a=1).to_broadcast([P, CE])
                     ).then_inc(self.far_loaded[k.u], 16)

    def maxima(self, dve, step, k, score):
        top, far = self.top[k.u], self.far[k.u]
        if k.start:
            step(dve.memset(top[:, 0:1], FAR))
        else:
            step(dve.tensor_copy(top[:, 0:1], self.top[1 - k.u][:, CE:CE + 1]))
        dve.wait_ge(self.far_loaded[k.u], 16 * (k.t + 1))
        step(dve.tensor_tensor_scan(top[:, 1:CE + 1], far[:], score, top[:, 0:1], ALU.add, ALU.max))
        dve.tensor_tensor(self.ex[:, 1, :], score, top[:, 1:CE + 1], ALU.subtract)
        step(dve.tensor_tensor(self.ex[:, 0, :], top[:, 0:CE], far[:], ALU.add))
        dve.sem_inc(self.far_used, 1)
        step(dve.tensor_tensor(self.ex[:, 0, :], self.ex[:, 0, :], top[:, 1:CE + 1], ALU.subtract))
        dve.sem_inc(self.shifted, 1)

    def exps(self, act, n):
        act.wait_ge(self.shifted, n)
        act.activation(self.ex[:], self.ex[:], ACT.Exp).then_inc(self.exped, 1)

    def add_up(self, dve, step, k, weigh):
        dve.wait_ge(self.exped, k.n)
        step(weigh(self.ex[0:D, 1, :]))
        step(dve.tensor_tensor_scan(self.sums[k.u][:], self.ex[:, 0, :], self.ex[:, 1, :],
                                    0.0 if k.start else self.sums[1 - k.u][:, CE - 1:CE], ALU.mult, ALU.add))
        dve.sem_inc(self.summed, 1)

    def turn(self, pe, c, k):
        pe.wait_ge(self.summed, k.n)
        for j in range(TPC):
            ins = pe.transpose(self.p_sums[:, j * P:(j + 1) * P], self.sums[k.u][:, j * P:(j + 1) * P], c.ident[:])
        ins.then_inc(self.sums_turned, 1)

    def divide(self, dve, step, n, out):
        dve.wait_ge(self.sums_turned, n)
        num, den = (self.p_sums[:].rearrange("p (j a h f) -> p j a h f", j=TPC, a=2, h=HEADS)[:, :, a] for a in range(2))
        step(dve.tensor_scalar(self.rden[:], den[:, :, :, 0], 1e-16, None, ALU.add))
        step(dve.reciprocal(self.rden[:], self.rden[:]))
        step(dve.tensor_tensor(out.rearrange("p j (h f) -> p j h f", h=HEADS), num,
                               self.rden[:].rearrange("p j (h o) -> p j h o", o=1).to_broadcast([P, TPC, HEADS, D // HEADS]), ALU.mult))


class Rows:

    def __init__(self, s, lists, width):
        self.lists = lists
        self.buf = [s.sb(f"rows{u}", [P, TPC, width]) for u in range(2)]
        self.num = [s.sb(f"num{u}", [P, len(lists), TPC], I32) for u in range(2)]
        self.gathered = [s.swdge_sem(f"gathered{u}") for u in range(2)]
        self.num_ready = s.sem("num_ready")
        self.rows_free = s.sem("rows_free")
        self.per = 16 * TPC * len(lists)

    def gather(self, pool, k):
        if not k.first:
            hold(pool, self.rows_free, k.n - 2)
        for m, (_, _, _, lst) in enumerate(self.lists):
            pool.tensor_copy(self.num[k.u][:, m, :], lst[:, bass.ds(k.i * TPC, TPC)]).then_inc(self.num_ready, 1)
        hold(pool, self.num_ready, k.n * len(self.lists))
        for m, (table, w, at, _) in enumerate(self.lists):
            for j in range(TPC):
                pool.indirect_dma_start(self.buf[k.u][:, j, at:at + w], None, table,
                                        bass.IndirectOffsetOnAxis(ap=self.num[k.u][:, m, j:j + 1], axis=0)
                                        ).then_inc(self.gathered[k.u], 16)

    def wait(self, eng, k):
        eng.wait_ge(self.gathered[k.u], self.per * (k.t + 1))


class Scatter:

    def __init__(self, s, table, width, lst, rows):
        self.table, self.lst, self.rows = table, lst, rows
        self.num = [s.sb(f"snum{u}", [P, TPC], I32) for u in range(2)]
        self.out = [s.sb(f"out{u}", [P, TPC, width]) for u in range(2)]
        self.scattered = [s.swdge_sem(f"scattered{u}") for u in range(2)]
        self.snum_ready, self.out_ready = s.sem("snum_ready"), s.sem("out_ready")

    def scatter(self, pool, k):
        if not k.first:
            hold(pool, self.scattered[k.u], 16 * TPC * k.t)
        pool.tensor_copy(self.num[k.u][:], self.lst[:, bass.ds(k.i * TPC, TPC)]).then_inc(self.snum_ready, 1)
        hold(pool, self.snum_ready, k.n)
        hold(pool, self.out_ready, k.n)
        for j in range(TPC):
            pool.indirect_dma_start(self.table, bass.IndirectOffsetOnAxis(ap=self.num[k.u][:, j:j + 1], axis=0),
                                    self.out[k.u][:, j, :], None, bounds_check=self.rows - 1, oob_is_err=False
                                    ).then_inc(self.scattered[k.u], 16)

    def free(self, eng, k):
        if not k.first:
            eng.wait_ge(self.scattered[k.u], 16 * TPC * k.t)

    def done(self, eng, turns):
        for u in range(2):
            eng.wait_ge(self.scattered[u], 16 * TPC * turns)


def gather_scatter(pool, c, rows, sct, lag):
    def body(*ks):
        if ks[0]:
            rows.gather(pool, ks[0])
        if sct and ks[lag]:
            sct.scatter(pool, ks[lag])
    slots(pool, c.NCH, lag if sct else 0, body)
    if sct:
        sct.done(pool, c.TURNS)


class EdgeAttr:

    def __init__(self, s, table, width, ones):
        self.table, self.w, self.ones = table, width, ones
        self.rows = [s.sb(f"ea{u}", [P, TPC, 32]) for u in range(2)]
        self.T = s.sb("eaT", [32, CE])
        self.p = s.ps("p_ea", (32, CE))
        self.loaded = [s.sem(f"ea_loaded{u}") for u in range(2)]
        self.turned, self.ready, self.cleared = s.sem("ea_turned"), s.sem("ea_ready"), s.sem("ea_cleared")

    def clear(self, eng):
        for u in range(2):
            eng.memset(self.rows[u][:], 1.0).then_inc(self.cleared, 1)

    def load(self, sp, c, k):
        if k.first:
            sp.wait_ge(self.cleared, 2)
        else:
            sp.wait_ge(self.turned, k.n - 2)
        at = slice(self.ones, self.ones + self.w)
        if not k.last:
            sp.dma_start(self.rows[k.u][:, :, at], edge_rows(self.table, k)).then_inc(self.loaded[k.u], 16)
            return
        base = (c.NCH - 1) * CE
        tiles, rest = (c.E - base) // P, (c.E - base) % P
        sp.dma_start(self.rows[k.u][:, 0:tiles, at],
                     self.table[base:base + tiles * P, :].rearrange("(j p) f -> p j f", p=P)).then_inc(self.loaded[k.u], 16)
        sp.dma_start(self.rows[k.u][0:rest, tiles, at], self.table[base + tiles * P:c.E, :]).then_inc(self.loaded[k.u], 16)

    def turn(self, pe, c, k):
        hold(pe, self.loaded[k.u], 16 * (k.t + 1) + (16 if k.last else 0))
        for j in range(TPC):
            ins = pe.transpose(self.p[0:32, j * P:(j + 1) * P], self.rows[k.u][:, j, :], c.ident[:])
        ins.then_inc(self.turned, 1)

    def copy_out(self, act, n):
        act.wait_ge(self.turned, n)
        act.activation(self.T[:], self.p[:], ACT.Copy).then_inc(self.ready, 1)


class Stats:

    def __init__(self, s):
        self.p = s.ps("p_stat", (P, CE))
        self.row = s.sb("stat_row", [1, P])
        self.b = s.sb("stat_b", [P, P])
        self.step, self.summed, self.row_out, self.spread = (s.sem("stat_" + n) for n in ("step", "summed", "row_out", "spread"))
        self.lnv, self.var = s.sb("stat_lnv", [P, D]), s.sb("stat_var", [P, D])
        self.ln_done, self.var_done = s.sem("stat_ln_done"), s.sem("stat_var_done")

    def begin(self, pe, c):
        pe.matmul(self.p[0:1, 0:P], c.zero_col[:, 0:1], c.ident[:], start=True, stop=False, skip_group_check=True)

    def add(self, pe, last, sums, done):
        for j in range(TPC):
            ins = pe.matmul(self.p[0:1, 0:P], last[:, j:j + 1], sums[:, j, :], start=False, stop=False, skip_group_check=True)
        ins.then_inc(done, 1)

    def finish(self, pe, c):
        pe.matmul(self.p[0:1, 0:P], c.zero_col[:, 0:1], c.ident[:], start=False, stop=True, skip_group_check=True).then_inc(self.summed, 1)
        pe.wait_ge(self.row_out, 1)
        pe.matmul(self.p[:, 2 * P:3 * P], c.ones_row[:], self.row[:], start=True, stop=True).then_inc(self.spread, 1)

    def scalar(self, act, c):
        act.wait_ge(self.var_done, 1)
        act.activation(self.lnv[:], self.var[:], ACT.Ln, bias=c.eps[:, 0:1]).then_inc(self.ln_done, 1)
        act.wait_ge(self.ln_done, 1)
        act.activation(self.lnv[:], self.lnv[:], ACT.Exp, scale=-0.5).then_inc(self.ln_done, 1)

    def vector(self, dve, c, gamma, beta, offset, scale, shift):
        step = Chain(dve, self.step)
        dve.wait_ge(self.summed, 1)
        step(dve.tensor_scalar(self.row[:], self.p[0:1, 0:P], 1.0 / c.N, None, ALU.mult))
        dve.sem_inc(self.row_out, 1)
        dve.wait_ge(self.spread, 1)
        step(dve.tensor_copy(self.b[:], self.p[:, 2 * P:3 * P]))
        mean, sq = self.b[:, 0:D], self.b[:, D:P]
        step(dve.tensor_tensor(self.lnv[:], mean, mean, ALU.mult))
        step(dve.tensor_tensor(self.var[:], sq, self.lnv[:], ALU.subtract))
        step(dve.tensor_scalar(self.var[:], self.var[:], 0.0, None, ALU.max))
        dve.sem_inc(self.var_done, 1)
        dve.wait_ge(self.ln_done, 2)
        step(dve.tensor_tensor(scale[:], self.lnv[:], gamma[:], ALU.mult))
        step(dve.tensor_tensor(mean, mean, offset[:], ALU.add))
        step(dve.tensor_tensor(mean, mean, scale[:], ALU.mult))
        step(dve.tensor_tensor(shift[:], beta[:], mean, ALU.subtract))


def edge_rows(table, k):
    return table[bass.ds(k.i * CE, CE), :].rearrange("(j p) f -> p j f", p=P)


def node_parts(c, k):
    rest = c.N - (c.NCH - 1) * P * NR
    assert rest % NR == 0 and 0 < rest <= P * NR
    return rest // NR if k.last else P


def node_rows(c, table, k, parts):
    return table[bass.ds(k.i * (P * NR), parts * NR), :].rearrange("(p r) f -> p r f", r=NR)


def tables_start(nc, c, x, tab1, tab2, consts):
    s = c.start
    s.xin = [s.sb(f"xin{u}", [P, NR, D]) for u in range(2)]
    s.row = [s.sb(f"row{u}", [P, NR, P]) for u in range(2)]
    s.tb = s.sb("tb", [P, D])
    s.fill = [s.sb(f"fill{q}", [P, NR, D]) for q in range(len(consts))]
    s.xin_loaded = [s.sem(f"xin_loaded{u}") for u in range(2)]
    s.stored = [s.sem(f"stored{u}") for u in range(2)]
    s.row_done, s.tanh_done, s.fixed, s.filled = (s.sem(n) for n in ("row_done", "tanh_done", "fixed", "filled"))

    def scalar(act):
        act.activation(s.tb[:], c.bias0[:], ACT.Tanh).then_inc(s.tanh_done, 1)

    def sync(sp):
        def body(k, old):
            if k:
                if not k.first:
                    sp.wait_ge(s.row_done, k.n - 2)
                parts = node_parts(c, k)
                sp.dma_start(s.xin[k.u][0:parts], node_rows(c, x, k, parts)).then_inc(s.xin_loaded[k.u], 16)
            if old:
                parts = node_parts(c, old)
                sp.wait_ge(s.row_done, old.n)
                sp.dma_start(node_rows(c, tab1, old, parts), s.row[old.u][0:parts, :, 0:D]).then_inc(s.stored[old.u], 16)
                sp.dma_start(node_rows(c, tab2, old, parts), s.row[old.u][0:parts]).then_inc(s.stored[old.u], 16)
                if old.start:
                    sp.wait_ge(s.fixed, 2 + len(consts))
                for q, (table, _) in enumerate(consts):
                    sp.dma_start(node_rows(c, table, old, parts), s.fill[q][0:parts]).then_inc(s.filled, 16)
        slots(sp, c.NCH, 1, body)
        for u in range(2):
            sp.wait_ge(s.stored[u], 32 * c.TURNS)
        sp.wait_ge(s.filled, 16 * len(consts) * c.NCH)

    def gpsimd(pool):
        for u in range(2):
            pool.tensor_copy(s.row[u][:, :, D:P], over_rows(c.bias1[:], NR)).then_inc(s.fixed, 1)
        for q, (_, row) in enumerate(consts):
            pool.tensor_copy(s.fill[q][:], over_rows(row[:], NR)).then_inc(s.fixed, 1)
        pool.wait_ge(s.tanh_done, 1)

        def body(k):
            parts = node_parts(c, k)
            pool.wait_ge(s.xin_loaded[k.u], 16 * (k.t + 1))
            if not k.first:
                hold(pool, s.stored[k.u], 32 * k.t)
            else:
                pool.nop(nofuse=True)
            pool.tensor_tensor(s.row[k.u][0:parts, :, 0:D], s.xin[k.u][0:parts], over_rows(s.tb[0:parts, :], NR),
                               ALU.add).then_inc(s.row_done, 1)
        slots(pool, c.NCH, 0, body)
    return scalar, sync, gpsimd


def two(ap):
    return ap.rearrange("p j (a f) -> p (j a) f", a=2)


def conv_gat(nc, c, x, dram, tab1):
    with Scope(nc, "l0") as s:
        rows = Rows(s, [(x, D, 0, c.idx_src), (x, D, D, c.idx_dst)], 2 * D)
        sct = Scatter(s, tab1, D, c.scat_d, c.N)
        norm = Norm(s, "n", 2 * TPC)
        sm = Softmax(s)
        h = s.sb("h", [P, TPC, 2 * D])
        hT = s.sb("hT", [P, CE])
        leak = s.sb("leak", [P, CE])
        res = s.sb("res", [P, TPC, D])
        e2, r2 = s.sb("e2", [P, TPC, D]), s.sb("r2", [P, TPC, D])
        x_one = [s.sb(f"x_one{u}", [P, TPC, D]) for u in range(2)]
        p_hT, p_val, p_score = s.ps("p_hT"), s.ps("p_val", (D, CE)), s.ps("p_score")
        m = s.sems("h_ready h_turned hT_ready scored valued leaked arg_ready exp2 clamped tanh_ready dve_step act_step x_kept")
        with nc.Block() as block:
            @block.sync
            def _(sp):
                slots(sp, c.NCH, 0, lambda k: sm.load(sp, k, dram["far_d"]))

            @block.gpsimd
            def _(pool):
                gather_scatter(pool, c, rows, sct, 3)

            @block.scalar
            def _(act):
                step = Chain(act, m["act_step"])
                load_ln_exp(nc, act)

                def body(k0, k1, k2):
                    if k0:
                        norm.square(act, k0.n)
                    if k2:
                        act.wait_ge(m["arg_ready"], k2.n)
                        act.activation(e2[:], res[:], ACT.Exp, scale=2.0).then_inc(m["exp2"], 1)
                    if k0:
                        norm.rsqrt(act, step, c, k0.n)
                        act.wait_ge(m["h_turned"], k0.n)
                        act.activation(hT[:], p_hT[:], ACT.Copy).then_inc(m["hT_ready"], 1)
                    if k2:
                        act.wait_ge(m["clamped"], k2.n)
                        step(act.activation(r2[:], e2[:], ACT.Ln, bias=c.one[:, 0:1]))
                        act.activation(r2[:], r2[:], ACT.Exp, scale=-1.0).then_inc(m["tanh_ready"], 1)
                    if k1:
                        sm.exps(act, k1.n)
                    if k0:
                        if not k0.first:
                            act.wait_ge(sct.out_ready, k0.n - 2)
                        act.activation(x_one[k0.u][:], rows.buf[k0.u][:, :, D:P], ACT.Identity, bias=c.one[:, 0:1]).then_inc(m["x_kept"], 1)
                        act.wait_ge(m["x_kept"], k0.n)
                        act.sem_inc(rows.rows_free, 1)
                        act.wait_ge(m["scored"], k0.n)
                        act.activation(leak[:], p_score[:], ACT.Copy, scale=0.2).then_inc(m["leaked"], 1)
                slots(act, c.NCH, 2, body, step)

            @block.vector
            def _(dve):
                step = Chain(dve, m["dve_step"])

                def body(k0, k1, k2):
                    if k0:
                        rows.wait(dve, k0)
                        norm.center(dve, step, two(rows.buf[k0.u][:]))
                    if k2:
                        sm.divide(dve, step, k2.n, res[:])
                        step(dve.tensor_tensor(res[:], res[:], over_rows(c.bias0[:], TPC), ALU.add))
                        dve.sem_inc(m["arg_ready"], 1)
                    if k0:
                        norm.add_up(dve, step, k0.n)
                        if not k0.start:
                            dve.wait_ge(m["h_turned"], k0.n - 1)
                        norm.scale(dve, step, k0.n, two(h[:]))
                        dve.sem_inc(m["h_ready"], 1)
                    if k2:
                        dve.wait_ge(m["exp2"], k2.n)
                        step(dve.tensor_scalar(e2[:], e2[:], BIG, None, ALU.min))
                        dve.sem_inc(m["clamped"], 1)
                    if k1:
                        dve.wait_ge(m["leaked"], k1.n)
                        step(dve.tensor_tensor(leak[:], p_score[:], leak[:], ALU.max))
                        sm.maxima(dve, step, k1, leak[:])
                    if k2:
                        sct.free(dve, k2)
                        dve.wait_ge(m["tanh_ready"], k2.n)
                        step(dve.scalar_tensor_tensor(sct.out[k2.u][:], r2[:], -2.0, x_one[k2.u][:], ALU.mult, ALU.add))
                        dve.sem_inc(sct.out_ready, 1)
                    if k1:
                        dve.wait_ge(m["valued"], k1.n)
                        sm.add_up(dve, step, k1, lambda p_: dve.tensor_tensor(p_, p_, p_val[:], ALU.mult))
                slots(dve, c.NCH, 2, body, step)

            @block.tensor
            def _(pe):
                def body(k0, k1):
                    if k0:
                        pe.wait_ge(m["h_ready"], k0.n)
                        for j in range(TPC):
                            ins = pe.transpose(p_hT[:, j * P:(j + 1) * P], h[:, j, :], c.ident[:])
                        ins.then_inc(m["h_turned"], 1)
                        hold(pe, m["hT_ready"], k0.n)
                        if k1:
                            hold(pe, sm.shifted, k1.n)
                        pe.matmul(p_score[:], c.w_att0[:], hT[:], start=True, stop=True).then_inc(m["scored"], 1)
                    if k1:
                        sm.turn(pe, c, k1)
                    if k0:
                        pe.matmul(p_val[:], c.w_val0[:], hT[0:D, :], start=True, stop=True).then_inc(m["valued"], 1)
                slots(pe, c.NCH, 1, body)


def conv_gatv2(nc, c, dram, x1, x1o, edge_attr):
    with Scope(nc, "l1") as s:
        rows = Rows(s, [(x1, D, 0, c.idx_src), (x1, D, D, c.idx_dst)], 2 * D)
        sct = Scatter(s, x1o, 2 * D, c.scat_d, c.N)
        norm = Norm(s, "n", 2 * TPC)
        sm = Softmax(s)
        h = s.sb("h", [P, TPC, 2 * D])
        hT = s.sb("hT", [P, CE])
        ea = EdgeAttr(s, edge_attr, 16, 0)
        g = s.sb("g", [P, CE])
        sums = s.sb("sums_sq", [P, TPC, 2 * D])
        last = s.sb("last", [P, TPC])
        x_keep = [s.sb(f"x_keep{u}", [P, TPC, D]) for u in range(2)]
        stat = Stats(s)
        p_hT, p_g, p_val, p_score = s.ps("p_hT"), s.ps("p_g"), s.ps("p_val", (D, CE)), s.ps("p_score")
        m = s.sems("h_ready h_turned hT_ready g_summed g_ready scored valued dve_step act_step squares sums_ready sums_added x_kept x_out")
        with nc.Block() as block:
            @block.sync
            def _(sp):
                def body(k):
                    sm.load(sp, k, dram["far_d"])
                    ea.load(sp, c, k)
                slots(sp, c.NCH, 0, body)

            @block.gpsimd
            def _(pool):
                ea.clear(pool)
                gather_scatter(pool, c, rows, sct, 3)

            @block.scalar
            def _(act):
                step = Chain(act, m["act_step"])
                load_ln_exp(nc, act)

                def body(k0, k1, k2):
                    if k0:
                        norm.square(act, k0.n)
                    if k2:
                        act.wait_ge(m["squares"], k2.n)
                        act.activation(sums[:, :, D:P], sums[:, :, 0:D], ACT.Square).then_inc(m["sums_ready"], 1)
                        sct.free(act, k2)
                        act.activation(sct.out[k2.u][:, :, 0:D], x_keep[k2.u][:], ACT.Copy).then_inc(m["x_out"], 1)
                    if k0:
                        norm.rsqrt(act, step, c, k0.n)
                        if not k0.first:
                            act.wait_ge(m["x_out"], k0.n - 2)
                        act.activation(x_keep[k0.u][:], rows.buf[k0.u][:, :, D:P], ACT.Copy).then_inc(m["x_kept"], 1)
                        act.wait_ge(m["x_kept"], k0.n)
                        act.sem_inc(rows.rows_free, 1)
                        ea.copy_out(act, k0.n)
                        act.wait_ge(m["h_turned"], k0.n)
                        act.activation(hT[:], p_hT[:], ACT.Copy).then_inc(m["hT_ready"], 1)
                    if k1:
                        sm.exps(act, k1.n)
                    if k0:
                        act.wait_ge(m["g_summed"], k0.n)
                        act.activation(g[0:D, :], p_g[0:D, :], ACT.Identity, bias=c.b_g1[0:D, 0:1])
                        act.activation(g[D:P, :], p_g[D:P, :], ACT.Relu, bias=c.b_g1[D:P, 0:1]).then_inc(m["g_ready"], 1)
                slots(act, c.NCH, 2, body, step)
                stat.scalar(act, c)

            @block.vector
            def _(dve):
                step = Chain(dve, m["dve_step"])

                def body(k0, k1, k2):
                    if k0:
                        rows.wait(dve, k0)
                        norm.center(dve, step, two(rows.buf[k0.u][:]))
                    if k2:
                        if not k2.start:
                            dve.wait_ge(m["sums_added"], k2.n - 1)
                        step(dve.tensor_copy(last[:], c.last_d[:, bass.ds(k2.i * TPC, TPC)]))
                        sm.divide(dve, step, k2.n, sums[:, :, 0:D])
                        dve.sem_inc(m["squares"], 1)
                    if k0:
                        norm.add_up(dve, step, k0.n)
                        if not k0.start:
                            dve.wait_ge(m["h_turned"], k0.n - 1)
                        norm.scale(dve, step, k0.n, two(h[:]))
                        dve.sem_inc(m["h_ready"], 1)
                    if k2:
                        dve.wait_ge(m["x_out"], k2.n)
                        step(dve.tensor_tensor(sct.out[k2.u][:, :, D:P], sums[:, :, 0:D], over_rows(c.bias1[:], TPC), ALU.add))
                        dve.sem_inc(sct.out_ready, 1)
                    if k1:
                        dve.wait_ge(m["scored"], k1.n)
                        sm.maxima(dve, step, k1, p_score[:])
                        dve.wait_ge(m["valued"], k1.n)
                        sm.add_up(dve, step, k1, lambda p_: dve.scalar_tensor_tensor(
                            p_, p_val[:], c.b_l1[:, 0:1], p_, ALU.add, ALU.mult))
                slots(dve, c.NCH, 2, body, step)
                stat.vector(dve, c, c.gamma1, c.beta1, c.bias1, c.scale1, c.shift1)

            @block.tensor
            def _(pe):
                stat.begin(pe, c)

                def body(k0, k1, k2):
                    if k0:
                        ea.turn(pe, c, k0)
                    if k2:
                        hold(pe, m["sums_ready"], k2.n)
                        stat.add(pe, last, sums, m["sums_added"])
                    if k0:
                        pe.wait_ge(m["h_ready"], k0.n)
                        for j in range(TPC):
                            ins = pe.transpose(p_hT[:, j * P:(j + 1) * P], h[:, j, :], c.ident[:])
                        ins.then_inc(m["h_turned"], 1)
                        hold(pe, ea.ready, k0.n)
                        hold(pe, m["hT_ready"], k0.n)
                        pe.matmul(p_g[:], c.w_lr[:].rearrange("p a f -> p (a f)"), hT[:], start=True, stop=False)
                        pe.matmul(p_g[:], c.w_e1[:].rearrange("p a f -> p (a f)"), ea.T[0:16, :], start=False, stop=True).then_inc(m["g_summed"], 1)
                    if k1:
                        sm.turn(pe, c, k1)
                    if k0:
                        pe.matmul(p_val[:], c.w_lr[0:D, 0, :], hT[0:D, :], start=True, stop=True).then_inc(m["valued"], 1)
                        hold(pe, m["g_ready"], k0.n)
                        pe.matmul(p_score[:], c.w_att1[:], g[:], start=True, stop=True).then_inc(m["scored"], 1)
                slots(pe, c.NCH, 2, body)
                stat.finish(pe, c)


def nodes_second(nc, c, x1o, xh):
    with Scope(nc, "d2") as s:
        rin = [s.sb(f"rin{u}", [P, NR, P]) for u in range(2)]
        out = [s.sb(f"out{u}", [P, NR, P]) for u in range(2)]
        na, nb = Norm(s, "na", NR), Norm(s, "nb", NR)
        y, h1, x2 = (s.sb(n, [P, NR, D]) for n in ("y", "h1", "x2"))
        yb = [s.sb(f"yb{u}", [P, NR, D]) for u in range(2)]
        loaded = [s.sem(f"loaded{u}") for u in range(2)]
        stored = [s.sem(f"stored{u}") for u in range(2)]
        m = s.sems("done dve_step act_step pool_step bn_part bn_ready gelu_done x2_done")
        with nc.Block() as block:
            @block.sync
            def _(sp):
                def body(k, k1, old):
                    if k:
                        if not k.first:
                            sp.wait_ge(m["x2_done"], k.n - 2)
                        sp.dma_start(rin[k.u][0:node_parts(c, k)], node_rows(c, x1o, k, node_parts(c, k))).then_inc(loaded[k.u], 16)
                    if old:
                        sp.wait_ge(m["done"], old.n)
                        sp.dma_start(node_rows(c, xh, old, node_parts(c, old)), out[old.u][0:node_parts(c, old)]).then_inc(stored[old.u], 16)
                slots(sp, c.NCH, 2, body)
                for u in range(2):
                    sp.wait_ge(stored[u], 16 * c.TURNS)

            @block.gpsimd
            def _(pool):
                def body(k):
                    p = node_parts(c, k)
                    hold(pool, loaded[k.u], 16 * (k.t + 1))
                    if not k.first:
                        hold(pool, m["x2_done"], k.n - 2)
                    pool.tensor_tensor(yb[k.u][0:p], rin[k.u][0:p, :, D:P], over_rows(c.scale1[0:p, :], NR), ALU.mult).then_inc(m["pool_step"], 1)
                    hold(pool, m["pool_step"], k.n)
                    pool.tensor_tensor(yb[k.u][0:p], yb[k.u][0:p], over_rows(c.shift1[0:p, :], NR), ALU.add).then_inc(m["bn_part"], 1)
                slots(pool, c.NCH, 0, body)

            @block.vector
            def _(dve):
                step = Chain(dve, m["dve_step"])

                def body(k, old):
                    if k:
                        p = node_parts(c, k)
                        dve.wait_ge(loaded[k.u], 16 * (k.t + 1))
                        na.center(dve, step, rin[k.u][0:p, :, 0:D], p)
                    if old:
                        q = node_parts(c, old)
                        dve.wait_ge(m["gelu_done"], old.n)
                        if not old.first:
                            dve.wait_ge(stored[old.u], 16 * old.t)
                        x2 = out[old.u][0:q, :, 0:D]
                        step(dve.tensor_tensor(x2, y[0:q], rin[old.u][0:q, :, 0:D], ALU.add))
                        dve.sem_inc(m["x2_done"], 1)
                        nb.center(dve, step, x2, q)
                    if k:
                        na.add_up(dve, step, k.n, p)
                    if old:
                        nb.add_up(dve, step, old.n, q)
                    if k:
                        na.scale(dve, step, k.n, h1[0:p], p)
                        dve.wait_ge(m["bn_part"], k.n)
                        step(dve.tensor_tensor(y[0:p], yb[k.u][0:p], h1[0:p], ALU.add))
                        dve.sem_inc(m["bn_ready"], 1)
                    if old:
                        nb.scale(dve, step, old.n, out[old.u][0:q, :, D:P], q)
                        dve.sem_inc(m["done"], 1)
                slots(dve, c.NCH, 1, body, step)

            @block.scalar
            def _(act):
                step = Chain(act, m["act_step"])

                def body(k, old):
                    p, q = k and node_parts(c, k), old and node_parts(c, old)
                    if k:
                        na.square(act, k.n, p)
                    if old:
                        nb.square(act, old.n, q)
                    load_ln_exp(nc, act)
                    if k:
                        na.rsqrt(act, step, c, k.n, p)
                    if old:
                        nb.rsqrt(act, step, c, old.n, q)
                    if k:
                        act.wait_ge(m["bn_ready"], k.n)
                        act.activation(y[0:p], y[0:p], ACT.Gelu).then_inc(m["gelu_done"], 1)
                slots(act, c.NCH, 1, body, step)


PAYW = 2 * D + 4


def edge_qkv(nc, c, xh, pay, edge_attr):
    with Scope(nc, "l2") as s:
        rows = Rows(s, [(xh, P, 0, c.idx_src), (xh, P, P, c.idx_dst)], 4 * D)
        hT = s.sb("hT", [P, CE])
        h = s.sb("h", [P, TPC, P])
        ea = EdgeAttr(s, edge_attr, 18, 1)
        qk = s.sb("qk", [P, TPC, D])
        prod = s.sb("prod", [P, TPC, 4, 8])
        out = [s.sb(f"out{u}", [P, TPC, PAYW]) for u in range(2)]
        p_hT, p_qkv = s.ps("p_hT"), s.ps("p_qkv")
        stored = [s.sem(f"stored{u}") for u in range(2)]
        m = s.sems("h_turned hT_ready qkv_done qkv_out pay_ready h_ready dve_step")
        with nc.Block() as block:
            @block.sync
            def _(sp):
                def body(k, old, _):
                    if k:
                        ea.load(sp, c, k)
                    if old:
                        sp.wait_ge(m["pay_ready"], old.n)
                        sp.dma_start(edge_rows(pay, old), out[old.u][:]).then_inc(stored[old.u], 16)
                slots(sp, c.NCH, 2, body)
                for u in range(2):
                    sp.wait_ge(stored[u], 16 * c.TURNS)

            @block.gpsimd
            def _(pool):
                ea.clear(pool)
                gather_scatter(pool, c, rows, None, 0)

            @block.scalar
            def _(act):
                def body(k, old):
                    if k:
                        ea.copy_out(act, k.n)
                    if old:
                        if not old.first:
                            act.wait_ge(stored[old.u], 16 * old.t)
                        if not old.start:
                            act.wait_ge(m["pay_ready"], old.n - 1)
                        act.wait_ge(m["qkv_done"], old.n)
                        v = p_qkv[:].rearrange("p (j f) -> p j f", j=TPC)
                        act.activation(out[old.u][:, :, 0:D], v[:, :, D:P], ACT.Copy)
                        act.activation(qk[:], v[:, :, 0:D], ACT.Copy).then_inc(m["qkv_out"], 1)
                    if k:
                        act.wait_ge(m["h_turned"], k.n)
                        act.activation(hT[:], p_hT[:], ACT.Copy).then_inc(m["hT_ready"], 1)
                slots(act, c.NCH, 1, body)

            @block.vector
            def _(dve):
                step = Chain(dve, m["dve_step"])

                def body(k, old):
                    if k:
                        rows.wait(dve, k)
                        buf = rows.buf[k.u][:].rearrange("p j (a f) -> p j a f", a=2)
                        if not k.start:
                            dve.wait_ge(m["h_turned"], k.n - 1)
                        step(dve.tensor_copy(h[:].rearrange("p j (a f) -> p j a f", a=2), buf[:, :, :, D:P]))
                        dve.sem_inc(m["h_ready"], 1)
                        if not k.first:
                            dve.wait_ge(stored[k.u], 16 * k.t)
                        step(dve.tensor_copy(out[k.u][:, :, D + 4:PAYW], rows.buf[k.u][:, :, 0:D]))
                        dve.sem_inc(rows.rows_free, 1)
                    if old:
                        dve.wait_ge(m["qkv_out"], old.n)
                        step(dve.tensor_tensor(prod[:].rearrange("p j h f -> p j (h f)"), qk[:, :, 0:32], qk[:, :, 32:64], ALU.mult))
                        step(dve.tensor_reduce(out[old.u][:, :, D:D + 4], prod[:], AX, ALU.add))
                        dve.sem_inc(m["pay_ready"], 1)
                slots(dve, c.NCH, 1, body, step)

            @block.tensor
            def _(pe):
                def body(k):
                    ea.turn(pe, c, k)
                    pe.wait_ge(m["h_ready"], k.n)
                    for j in range(TPC):
                        ins = pe.transpose(p_hT[:, j * P:(j + 1) * P], h[:, j, :], c.ident[:])
                    ins.then_inc(m["h_turned"], 1)
                    hold(pe, m["hT_ready"], k.n)
                    hold(pe, ea.ready, k.n)
                    if not k.start:
                        hold(pe, m["qkv_out"], k.n - 1)
                    for j in range(TPC):
                        at = slice(j * P, (j + 1) * P)
                        pe.matmul(p_qkv[:, at], hT[:, at], c.w_qkv[:], start=True, stop=False)
                        ins = pe.matmul(p_qkv[:, at], ea.T[0:19, at], c.w_rpe[:], start=False, stop=True)
                    ins.then_inc(m["qkv_done"], 1)
                slots(pe, c.NCH, 0, body)


def conv_rpe(nc, c, dram, pay, xh):
    with Scope(nc, "l2s") as s:
        rows = Rows(s, [(pay, PAYW, 0, c.perm)], PAYW)
        sct = Scatter(s, xh, P, c.scat_s, c.N)
        sm = Softmax(s)
        norm = Norm(s, "n", TPC)
        vT = [s.sb(f"vT{u}", [D + 4, CE]) for u in range(2)]
        x_keep = [s.sb(f"x_keep{u}", [P, TPC, D]) for u in range(2)]
        p_vT, p_score = s.ps("p_vT", (D + 4, CE)), s.ps("p_score")
        m = s.sems("turned vT_ready scored dve_step act_step x_kept res_ready")
        with nc.Block() as block:
            @block.sync
            def _(sp):
                slots(sp, c.NCH, 0, lambda k: sm.load(sp, k, dram["far_s"]))

            @block.gpsimd
            def _(pool):
                gather_scatter(pool, c, rows, sct, 4)

            @block.scalar
            def _(act):
                step = Chain(act, m["act_step"])
                load_ln_exp(nc, act)

                def body(k0, k1, k2):
                    if k0:
                        act.wait_ge(m["turned"], k0.n)
                        act.activation(vT[k0.u][:], p_vT[:], ACT.Copy).then_inc(m["vT_ready"], 1)
                    if k1:
                        sm.exps(act, k1.n)
                    if k2:
                        norm.square(act, k2.n)
                    if k0:
                        if not k0.first:
                            act.wait_ge(norm.centered, k0.n - 2)
                        act.activation(x_keep[k0.u][:], rows.buf[k0.u][:, :, D + 4:PAYW], ACT.Copy).then_inc(m["x_kept"], 1)
                        act.wait_ge(m["x_kept"], k0.n)
                        act.sem_inc(rows.rows_free, 1)
                    if k2:
                        norm.rsqrt(act, step, c, k2.n)
                slots(act, c.NCH, 2, body, step)

            @block.vector
            def _(dve):
                step = Chain(dve, m["dve_step"])

                def body(k0, k1, k2):
                    if k1:
                        dve.wait_ge(m["scored"], k1.n)
                        sm.maxima(dve, step, k1, p_score[:])
                    if k2:
                        sct.free(dve, k2)
                        x3 = sct.out[k2.u][:, :, 0:D]
                        sm.divide(dve, step, k2.n, x3)
                        step(dve.tensor_tensor(x3, x3, x_keep[k2.u][:], ALU.add))
                        norm.center(dve, step, x3)
                    if k1:
                        sm.add_up(dve, step, k1, lambda p_: dve.tensor_tensor(p_, p_, vT[k1.u][0:D, :], ALU.mult))
                    if k2:
                        norm.add_up(dve, step, k2.n)
                        norm.scale(dve, step, k2.n, sct.out[k2.u][:, :, D:P])
                        dve.sem_inc(sct.out_ready, 1)
                slots(dve, c.NCH, 2, body, step)

            @block.tensor
            def _(pe):
                def body(k0, k1):
                    if k0:
                        hold(pe, rows.gathered[k0.u], rows.per * (k0.t + 1))
                        for j in range(TPC):
                            ins = pe.transpose(p_vT[:, j * P:(j + 1) * P], rows.buf[k0.u][:, j, 0:D + 4], c.ident[:])
                        ins.then_inc(m["turned"], 1)
                        hold(pe, m["vT_ready"], k0.n)
                        if k1:
                            hold(pe, sm.shifted, k1.n)
                        pe.matmul(p_score[:], c.w_head[:], vT[k0.u][:], start=True, stop=True).then_inc(m["scored"], 1)
                    if k1:
                        sm.turn(pe, c, k1)
                slots(pe, c.NCH, 1, body)


class Gru:

    def __init__(self, s, R):
        self.e = s.sb("gru_e", [P, R, P])
        self.a = s.sb("gru_a", [P, R, D])
        self.cand = s.sb("gru_cand", [P, R, D])
        self.gates_done, self.sigmoids, self.arg_ready, self.tanh_done = (
            s.sem("gru_" + n) for n in ("gates_done", "sigmoids", "arg_ready", "tanh_done"))

    def sigmoid(self, act, n, gates):
        act.wait_ge(self.gates_done, n)
        act.activation(self.e[:], gates[:, :, 0:P], ACT.Sigmoid).then_inc(self.sigmoids, 1)

    def tanh(self, act, n):
        act.wait_ge(self.arg_ready, n)
        act.activation(self.cand[:], self.a[:], ACT.Tanh).then_inc(self.tanh_done, 1)

    def reset(self, dve, step, n, gates):
        dve.wait_ge(self.sigmoids, n)
        step(dve.tensor_tensor(self.a[:], self.e[:, :, 0:D], gates[:, :, 3 * D:4 * D], ALU.mult))
        step(dve.tensor_tensor(self.a[:], self.a[:], gates[:, :, 2 * D:3 * D], ALU.add))
        dve.sem_inc(self.arg_ready, 1)

    def update(self, dve, step, n, state, out):
        e, a, cand = self.e, self.a, self.cand
        dve.wait_ge(self.tanh_done, n)
        if state is None:
            step(dve.tensor_tensor(a[:], e[:, :, D:P], cand[:], ALU.mult))
            step(dve.tensor_tensor(out, cand[:], a[:], ALU.subtract))
        else:
            step(dve.tensor_tensor(a[:], state, cand[:], ALU.subtract))
            step(dve.tensor_tensor(a[:], a[:], e[:, :, D:P], ALU.mult))
            step(dve.tensor_tensor(out, cand[:], a[:], ALU.add))


def quiet_states(nc, c):
    c.quiet = [c.scope.sb(f"quiet{k}", [P, D]) for k in range(2)]
    with Scope(nc, "q") as s:
        st = s.sb("st", [P, P])
        p_g, p_t = s.ps("p_g"), s.ps("p_t")
        gru = Gru(s, 1)
        dve_step, turned, q_ready, st_ready = s.sem("dve_step"), s.sem("turned"), s.sem("q_ready"), s.sem("st_ready")
        pair = s.sb("pair", [P, P])
        gates = p_g[:, 0:4 * D].rearrange("p (a f) -> p a f", a=1)
        with nc.Block() as block:
            @block.tensor
            def _(pe):
                for k in range(2):
                    if k:
                        pe.wait_ge(q_ready, 1)
                        pe.transpose(p_t[:, 0:P], pair[:], c.ident[:]).then_inc(turned, 1)
                        pe.wait_ge(st_ready, 1)
                        pe.matmul(gates[:, 0, :], st[:], c.w_gate[:], start=True, stop=False)
                    pe.matmul(gates[:, 0, :], c.ones_row[:], c.b_gate[:], start=not k, stop=True).then_inc(gru.gates_done, 1)

            @block.scalar
            def _(act):
                for k in range(2):
                    gru.sigmoid(act, k + 1, gates)
                    gru.tanh(act, k + 1)

            @block.vector
            def _(dve):
                step = Chain(dve, dve_step)
                step(dve.memset(pair[:], 0.0))
                for k in range(2):
                    one = lambda q: q[:].rearrange("p (a f) -> p a f", a=1)
                    if k:
                        step(dve.tensor_copy(pair[:, D:P], c.quiet[0][:]))
                        dve.sem_inc(q_ready, 1)
                        dve.wait_ge(turned, 1)
                        step(dve.tensor_copy(st[:], p_t[:, 0:P]))
                        dve.sem_inc(st_ready, 1)
                    gru.reset(dve, step, k + 1, gates)
                    gru.update(dve, step, k + 1, one(c.quiet[0]) if k else None, one(c.quiet[k]))


def conv_rgcn(nc, c, name, dram, table, k_, g_rows, out_table):
    with Scope(nc, name) as s:
        width, at = (P, D) if k_ == 0 else (D, 0)
        rows = Rows(s, [(table, width, 0, c.idx_src)], width)
        sct = Scatter(s, out_table, D, c.scat_d, c.N)
        keep = [s.sb(f"keep{u}", [D, CE]) for u in range(2)]
        hm = s.sb("hm", [P, TPC, 2 * D])
        st_rows = [s.sb(f"st_rows{u}", [P, TPC, D]) for u in range(2)]
        st_keep = [s.sb(f"st_keep{u}", [P, TPC, D]) for u in range(2)]
        h01, h2 = s.sb("h01", [P, CE]), s.sb("h2", [D, CE])
        acc = [s.sb(f"acc{u}", [P, CE]) for u in range(2)]
        pair = s.sb("pair", [P, TPC, P])
        gru = Gru(s, TPC)
        stat = Stats(s) if k_ else None
        sums = s.sb("sums", [P, TPC, P])
        last = s.sb("last", [P, TPC])
        w = s.sb("w", [P, TPC, c.NREL])
        p_01, p_2, p_msg, p_gate = s.ps("p_01"), s.ps("p_2"), s.ps("p_msg", (D, CE)), s.ps("p_gate", (P, 2 * CE))
        gates = p_gate[:].rearrange("p (j f) -> p j f", j=TPC)
        keep_loaded = [s.sem(f"keep_loaded{u}") for u in range(2)]
        st_loaded = [s.sem(f"st_loaded{u}") for u in range(2)]
        g_stored = [s.sem(f"g_stored{u}") for u in range(2)]
        m = s.sems("hm_ready turned h_out msg_done acc_ready sums_ready sums_added dve_step reset_done squares")
        with nc.Block() as block:
            @block.sync
            def _(sp):
                def body(k, _, old):
                    if k:
                        if not k.first:
                            sp.wait_ge(m["acc_ready"], k.n - 2)
                        sp.dma_start(keep[k.u][:], dram["keep_d"][bass.ds(k.i * CE, CE)].rearrange("(a f) -> a f", a=1).to_broadcast([D, CE])
                                     ).then_inc(keep_loaded[k.u], 16)
                        if k_:
                            sp.dma_start(st_rows[k.u][:], edge_rows(g_rows, k)).then_inc(st_loaded[k.u], 16)
                    if old and k_ == 0:
                        sp.wait_ge(sct.out_ready, old.n)
                        sp.dma_start(edge_rows(g_rows, old), sct.out[old.u][:]).then_inc(g_stored[old.u], 16)
                slots(sp, c.NCH, 2, body)
                if k_ == 0:
                    for u in range(2):
                        sp.wait_ge(g_stored[u], 16 * c.TURNS)

            @block.gpsimd
            def _(pool):
                gather_scatter(pool, c, rows, sct, 3)

            @block.scalar
            def _(act):
                def body(k0, k1, k2):
                    if k0:
                        act.wait_ge(m["turned"], k0.n)
                        act.activation(h01[:], p_01[:], ACT.Copy)
                        if k_:
                            act.activation(acc[k0.u][D:P, :], p_2[D:P, :], ACT.Copy)
                        act.activation(h2[:], p_2[0:D, :], ACT.Copy).then_inc(m["h_out"], 1)
                    if k2 and stat:
                        act.wait_ge(m["squares"], k2.n)
                        act.activation(sums[:, :, D:P], sums[:, :, 0:D], ACT.Square).then_inc(m["sums_ready"], 1)
                    if k1:
                        if not k1.start:
                            act.wait_ge(sct.out_ready, k1.n - 1)
                        gru.sigmoid(act, k1.n, gates)
                        gru.tanh(act, k1.n)
                slots(act, c.NCH, 2, body)
                if stat:
                    stat.scalar(act, c)

            @block.vector
            def _(dve):
                step = Chain(dve, m["dve_step"])
                if k_ == 0:
                    step(dve.memset(pair[:], 0.0))
                    for u in range(2):
                        step(dve.memset(acc[u][D:P, :], 0.0))

                def body(k0, k1, k2):
                    if k0:
                        buf = rows.buf[k0.u][:, :, at:at + D]
                        step(dve.tensor_copy(w[:], c.wrel[:, bass.ds(k0.i * TPC, TPC), :]))
                        rows.wait(dve, k0)
                        for r, o in enumerate((hm[:, :, 0:D], hm[:, :, D:P], pair[:, :, 0:D])):
                            ins = dve.tensor_tensor(o, buf, rows4(w[:, :, r]), ALU.mult)
                        step(ins)
                        if k_:
                            dve.wait_ge(st_loaded[k0.u], 16 * (k0.t + 1))
                            step(dve.tensor_copy(pair[:, :, D:P], st_rows[k0.u][:]))
                        dve.sem_inc(m["hm_ready"], 1)
                        dve.sem_inc(rows.rows_free, 1)
                    if k2:
                        sct.free(dve, k2)
                        if k_ == 0 and not k2.first:
                            dve.wait_ge(g_stored[k2.u], 16 * k2.t)
                        gru.update(dve, step, k2.n, st_keep[k2.u][:] if k_ else None, sct.out[k2.u][:])
                        dve.sem_inc(sct.out_ready, 1)
                    if k0 and k_:
                        step(dve.tensor_copy(st_keep[k0.u][:], st_rows[k0.u][:]))
                    if k2 and stat:
                        if not k2.start:
                            dve.wait_ge(m["sums_added"], k2.n - 1)
                        step(dve.tensor_copy(last[:], c.last_d[:, bass.ds(k2.i * TPC, TPC)]))
                        step(dve.tensor_tensor(sums[:, :, 0:D], sct.out[k2.u][:], over_rows(c.quiet[1][:], TPC), ALU.subtract))
                        dve.sem_inc(m["squares"], 1)
                    if k1:
                        gru.reset(dve, step, k1.n, gates)
                        dve.sem_inc(m["reset_done"], 1)
                    if k0:
                        dve.wait_ge(keep_loaded[k0.u], 16 * (k0.t + 1))
                        dve.wait_ge(m["msg_done"], k0.n)
                        step(dve.tensor_tensor_scan(acc[k0.u][0:D, :], keep[k0.u][:], p_msg[:],
                                                    0.0 if k0.start else acc[1 - k0.u][0:D, CE - 1:CE], ALU.mult, ALU.add))
                        dve.sem_inc(m["acc_ready"], 1)
                slots(dve, c.NCH, 2, body, step)
                if stat:
                    stat.vector(dve, c, c.gamma3, c.beta3, c.quiet[1], c.scale3, c.shift3)

            @block.tensor
            def _(pe):
                if stat:
                    stat.begin(pe, c)

                def body(k0, k1, k2):
                    if k0:
                        hold(pe, m["hm_ready"], k0.n)
                        for j in range(TPC):
                            cols = slice(j * P, (j + 1) * P)
                            pe.transpose(p_01[:, cols], hm[:, j, 0:P], c.ident[:])
                            ins = pe.transpose(p_2[:, cols], pair[:, j, :], c.ident[:])
                        ins.then_inc(m["turned"], 1)
                    if k1:
                        hold(pe, m["acc_ready"], k1.n)
                        if not k1.start:
                            hold(pe, m["reset_done"], k1.n - 1)
                        for j in range(TPC):
                            pe.matmul(gates[:, j, :], acc[k1.u][:, j * P:(j + 1) * P], c.w_gate[:], start=True, stop=False)
                            ins = pe.matmul(gates[:, j, :], c.ones_row[:], c.b_gate[:], start=False, stop=True)
                        ins.then_inc(gru.gates_done, 1)
                    if k0:
                        hold(pe, m["h_out"], k0.n)
                        pe.matmul(p_msg[:], c.w_rel01[:], h01[:], start=True, stop=False)
                        pe.matmul(p_msg[:], c.w_rel2[:], h2[:], start=False, stop=True).then_inc(m["msg_done"], 1)
                    if k2 and stat:
                        hold(pe, m["sums_ready"], k2.n)
                        stat.add(pe, last, sums, m["sums_added"])
                slots(pe, c.NCH, 2, body)
                if stat:
                    stat.finish(pe, c)


def nodes_last(nc, c, xh, g2, out):
    with Scope(nc, "dl") as s:
        xin = [s.sb(f"xin{u}", [P, NR, D]) for u in range(2)]
        gin = [s.sb(f"gin{u}", [P, NR, D]) for u in range(2)]
        res = [s.sb(f"res{u}", [P, NR, D]) for u in range(2)]
        loaded = [s.sem(f"loaded{u}") for u in range(2)]
        stored = [s.sem(f"stored{u}") for u in range(2)]
        done, dve_step, pool_done = s.sem("done"), s.sem("dve_step"), s.sem("pool_done")
        with nc.Block() as block:
            @block.sync
            def _(sp):
                def body(k):
                    p = node_parts(c, k)
                    if not k.first:
                        sp.wait_ge(done, k.n - 2)
                    sp.dma_start(xin[k.u][0:p], node_rows(c, xh, k, p)[:, :, 0:D]).then_inc(loaded[k.u], 16)
                    sp.dma_start(gin[k.u][0:p], node_rows(c, g2, k, p)).then_inc(loaded[k.u], 16)
                slots(sp, c.NCH, 0, body)

            @block.scalar
            def _(act):
                def body(k):
                    p = node_parts(c, k)
                    act.wait_ge(done, k.n)
                    act.dma_start(node_rows(c, out, k, p), res[k.u][0:p]).then_inc(stored[k.u], 16)
                slots(act, c.NCH, 0, body)
                for u in range(2):
                    act.wait_ge(stored[u], 16 * c.TURNS)

            @block.gpsimd
            def _(pool):
                def body(k):
                    p = node_parts(c, k)
                    hold(pool, loaded[k.u], 32 * (k.t + 1))
                    pool.tensor_tensor(xin[k.u][0:p], xin[k.u][0:p], over_rows(c.shift3[0:p, :], NR), ALU.add).then_inc(pool_done, 1)
                slots(pool, c.NCH, 0, body)

            @block.vector
            def _(dve):
                step = Chain(dve, dve_step)

                def body(k):
                    p = node_parts(c, k)
                    dve.wait_ge(loaded[k.u], 32 * (k.t + 1))
                    if not k.first:
                        dve.wait_ge(stored[k.u], 16 * k.t)
                    r = res[k.u][0:p]
                    step(dve.tensor_tensor(r, gin[k.u][0:p], over_rows(c.scale3[0:p, :], NR), ALU.mult))
                    dve.wait_ge(pool_done, k.n)
                    step(dve.tensor_tensor(r, r, xin[k.u][0:p], ALU.add))
                    dve.sem_inc(done, 1)
                slots(dve, c.NCH, 0, body, step)


class Common:
    pass


def gnn(nc, a, out):
    c = Common()
    E, N = a["src"].shape[0], a["x"].shape[0]
    c.E, c.N, c.NREL = E, N, a["L3_gnn_weight"].shape[0]
    c.NCH = -(-E // CE)
    c.NT = c.NCH * TPC
    c.TURNS = c.NCH // 2
    assert c.NCH % 2 == 0 and c.NT * P <= LIST and N < PAD_NODE and N <= SKIP and c.NREL == 3

    def table(name, shape):
        return nc.dram_tensor(name, shape, F32, kind="Internal").ap()

    dram = {"keys": table("keys", (LIST + 2,)), "far_d": table("far_d", (LIST,)),
            "keep_d": table("keep_d", (LIST,)), "far_s": table("far_s", (LIST,))}
    x1, x1o, xh = table("x1", (N, D)), table("x1o", (N, 2 * D)), table("xh", (N, 2 * D))
    pay, g_rows = table("pay", (c.NCH * CE, PAYW)), table("g_rows", (c.NCH * CE, D))
    g1, g2 = table("g1", (N, D)), table("g2", (N, D))
    with Scope(nc, "all") as sc:
        c.scope = Scope.whole = sc
        c.ident = sc.sb("ident", [P, P])
        c.minus1 = sc.sb("minus1", [1, 1])
        c.idx_src, c.idx_dst, c.scat_d, c.scat_s, c.perm = (
            sc.sb(name, [P, c.NT], I32) for name in ("idx_src", "idx_dst", "scat_d", "scat_s", "perm"))
        c.last_d = sc.sb("last_d", [P, c.NT])
        c.wrel = sc.sb("wrel", [P, c.NT, c.NREL])
        c.eps, c.one = sc.sb("eps", [P, 1]), sc.sb("one", [P, 1])
        setup(nc, c, a)
        quiet_states(nc, c)
        with Scope(nc, "ts") as c.start:
            beside = tables_start(nc, c, a["x"], x1, x1o, [(g1, c.quiet[0]), (g2, c.quiet[1])])
            prep_lists(nc, c, a["src"], a["dst"], a["edge_weight"], a["edge_type_3"], dram, beside)
        conv_gat(nc, c, a["x"], dram, x1)
        conv_gatv2(nc, c, dram, x1, x1o, a["edge_attr_16"])
        nodes_second(nc, c, x1o, xh)
        edge_qkv(nc, c, xh, pay, a["edge_attr_18"])
        conv_rpe(nc, c, dram, pay, xh)
        conv_rgcn(nc, c, "l3a", dram, xh, 0, g_rows, g1)
        conv_rgcn(nc, c, "l3b", dram, g1, 1, g_rows, g2)
        nodes_last(nc, c, xh, g2, out)


def kernel(**inputs):
    import numpy as np
    import concourse.bacc as bacc
    from concourse.bass_utils import run_bass_kernel_spmd as run

    nc = bacc.Bacc("TRN2", target_bir_lowering=False, num_devices=1)
    arrays = {f"in_{k}": np.ascontiguousarray(v) for k, v in inputs.items()}
    ins = {k: nc.dram_tensor(f"in_{k}", arrays[f"in_{k}"].shape, mybir.dt.from_np(arrays[f"in_{k}"].dtype),
                             kind="ExternalInput").ap() for k in inputs}
    out = nc.dram_tensor("out_0", inputs["x"].shape, F32, kind="ExternalOutput").ap()
    gnn(nc, ins, out)
    return run(nc, [arrays], core_ids=[0]).results[0]["out_0"]
```
